# Optimizing a Trainium2 kernel written in Bass

```python
import numpy as np
import jax
import jax.numpy as jnp

def _softmax(x, axis=-1):
    return jax.nn.softmax(x, axis=axis)

def _gelu(x):
    return jax.nn.gelu(x, approximate=True)

def _silu(x):
    return jax.nn.silu(x)

def _sigmoid(x):
    return jax.nn.sigmoid(x)

def _layernorm(x, axis=-1, eps=1e-05):
    m = jnp.mean(x, axis=axis, keepdims=True)
    v = jnp.var(x, axis=axis, keepdims=True)
    return (x - m) / jnp.sqrt(v + eps)

def _scatter_add(tgt, idx, src, axis=0):
    return tgt.at[idx].add(src)

def _segment_sum(src, seg, n):
    return jax.ops.segment_sum(src, seg, n)
kernel_name = 'mk_adj_resnorm_d4_adj_r2_7730d7'

def setup_inputs(seed: int=0):
    np.random.seed(seed)
    _w = jnp.asarray

    def _rec_inputs():
        import jax
        import jax.numpy as jnp
        _gk = jax.random.key(seed)
        x = -0.0005207 + 1.001 * jax.random.normal(jax.random.fold_in(_gk, 1), (8, 1024, 128), jnp.float32)
        _a = jax.random.bernoulli(jax.random.fold_in(_gk, 2), 0.015625, (1024, 1024))
        _a = jnp.logical_or(_a, jnp.swapaxes(_a, -1, -2))
        _a = jnp.logical_or(_a, jnp.eye(1024, dtype=bool))
        adj = _a.astype(jnp.int32)
        return (x, adj)
    x, adj = _rec_inputs()

    def _L0_gnn_setup():
        import jax, jax.numpy as jnp
        import numpy as np
        import math
        CHUNK = 128
        NUM_HEADS = 4
        EPS = 1e-05
        key = jax.random.key(seed)
        ks = jax.random.split(key, 12)
        B, N, F = (4, 1024, 128)
        x = jax.random.normal(ks[0], (B, N, F), dtype=jnp.float32)
        adj_matrix = jax.random.randint(ks[1], (N, N), 0, 2, dtype=jnp.int32)
        s = 1.0 / math.sqrt(F)
        Wq = jax.random.normal(ks[2], (F, F), dtype=jnp.float32) * s
        bq = jnp.zeros((F,), dtype=jnp.float32)
        Wk = jax.random.normal(ks[3], (F, F), dtype=jnp.float32) * s
        bk = jnp.zeros((F,), dtype=jnp.float32)
        Wv = jax.random.normal(ks[4], (F, F), dtype=jnp.float32) * s
        bv = jnp.zeros((F,), dtype=jnp.float32)
        Wo = jax.random.normal(ks[5], (F, F), dtype=jnp.float32) * s
        bo = jnp.zeros((F,), dtype=jnp.float32)
        gamma = jnp.ones((F,), dtype=jnp.float32)
        beta = jnp.zeros((F,), dtype=jnp.float32)
        return {'x': x, 'adj_matrix': adj_matrix, 'Wq': Wq, 'bq': bq, 'Wk': Wk, 'bk': bk, 'Wv': Wv, 'bv': bv, 'Wo': Wo, 'bo': bo, 'gamma': gamma, 'beta': beta}
    _L0_gnn_all = _L0_gnn_setup()
    _L0_gnn_in = {k: v for k, v in _L0_gnn_all.items() if k in ('Wq', 'bq', 'Wk', 'bk', 'Wv', 'bv', 'Wo', 'bo', 'gamma', 'beta')}
    del _L0_gnn_all

    def _L1_gnn_setup():
        import jax, jax.numpy as jnp
        import numpy as np
        B, N, D_IN, D_OUT, H = (64, 256, 128, 128, 4)
        HD = D_OUT // H
        key = jax.random.key(seed)
        ks = jax.random.split(key, 10)
        x = jax.random.normal(ks[0], (B, N, D_IN), dtype=jnp.float32)
        adj = jax.random.randint(ks[1], (N, N), 0, 2, dtype=jnp.int32)
        adj = adj.at[jnp.arange(N), jnp.arange(N)].set(1)
        s_in = 1.0 / np.sqrt(D_IN)
        s_out = 1.0 / np.sqrt(D_OUT)
        wq = jax.random.uniform(ks[2], (D_OUT, D_IN), jnp.float32, -s_in, s_in)
        bq = jax.random.uniform(ks[3], (D_OUT,), jnp.float32, -s_in, s_in)
        wk = jax.random.uniform(ks[4], (D_OUT, D_IN), jnp.float32, -s_in, s_in)
        bk = jax.random.uniform(ks[5], (D_OUT,), jnp.float32, -s_in, s_in)
        wv = jax.random.uniform(ks[6], (D_OUT, D_IN), jnp.float32, -s_in, s_in)
        bv = jax.random.uniform(ks[7], (D_OUT,), jnp.float32, -s_in, s_in)
        wo = jax.random.uniform(ks[8], (D_OUT, D_OUT), jnp.float32, -s_out, s_out)
        bo = jax.random.uniform(ks[9], (D_OUT,), jnp.float32, -s_out, s_out)
        return {'x': x, 'adj': adj, 'wq': wq, 'bq': bq, 'wk': wk, 'bk': bk, 'wv': wv, 'bv': bv, 'wo': wo, 'bo': bo}
    _L1_gnn_all = _L1_gnn_setup()
    _L1_gnn_in = {k: v for k, v in _L1_gnn_all.items() if k in ('wq', 'bq', 'wk', 'bk', 'wv', 'bv', 'wo', 'bo')}
    del _L1_gnn_all

    def _L2_gnn_setup():
        import jax, jax.numpy as jnp
        import numpy as np
        LEAKY_ALPHA = 0.2
        key = jax.random.key(seed)
        k1, k2, k3, k4 = jax.random.split(key, 4)
        B, N, Fin, Fout = (8, 1024, 128, 128)
        h = jax.random.normal(k1, (B, N, Fin), dtype=jnp.float32)
        adj = jax.random.randint(k2, (N, N), 0, 2, dtype=jnp.int32)
        W = jax.random.normal(k3, (Fin, Fout), dtype=jnp.float32) * (1.414 * (6.0 / (Fin + Fout)) ** 0.5)
        a = jax.random.normal(k4, (2 * Fout, 1), dtype=jnp.float32) * (1.414 * (6.0 / (2 * Fout + 1)) ** 0.5)
        return {'h': h, 'adj': adj, 'W': W, 'a': a}
    _L2_gnn_all = _L2_gnn_setup()
    _L2_gnn_in = {k: v for k, v in _L2_gnn_all.items() if k in ('W', 'a')}
    del _L2_gnn_all

    def _L3_gnn_setup():
        import jax, jax.numpy as jnp
        import numpy as np
        ALPHA = 0.2
        MASK_VAL = -9000000000000000.0
        key = jax.random.key(seed)
        k1, k2, k3, k4 = jax.random.split(key, 4)
        B, N, F = (8, 512, 128)
        H, OUT = (4, 128)
        hs = OUT // H
        x = jax.random.normal(k1, (B, N, F), dtype=jnp.float32)
        adj = jax.random.randint(k2, (N, N), 0, 2, dtype=jnp.int32)
        wb = float(np.sqrt(6.0 / (F + hs)))
        ab = float(np.sqrt(6.0 / (H + 2 * hs)))
        W = jax.random.uniform(k3, (H, F, hs), dtype=jnp.float32, minval=-wb, maxval=wb)
        a = jax.random.uniform(k4, (H, 2 * hs), dtype=jnp.float32, minval=-ab, maxval=ab)
        return {'x': x, 'adj': adj, 'W': W, 'a': a}
    _L3_gnn_all = _L3_gnn_setup()
    _L3_gnn_in = {k: v for k, v in _L3_gnn_all.items() if k in ('W', 'a')}
    del _L3_gnn_all
    return {'x': x, 'adj': adj, 'L0_gnn_Wq': _L0_gnn_in['Wq'], 'L0_gnn_bq': _L0_gnn_in['bq'], 'L0_gnn_Wk': _L0_gnn_in['Wk'], 'L0_gnn_bk': _L0_gnn_in['bk'], 'L0_gnn_Wv': _L0_gnn_in['Wv'], 'L0_gnn_bv': _L0_gnn_in['bv'], 'L0_gnn_Wo': _L0_gnn_in['Wo'], 'L0_gnn_bo': _L0_gnn_in['bo'], 'L0_gnn_gamma': _L0_gnn_in['gamma'], 'L0_gnn_beta': _L0_gnn_in['beta'], 'L1_gnn_wq': _L1_gnn_in['wq'], 'L1_gnn_bq': _L1_gnn_in['bq'], 'L1_gnn_wk': _L1_gnn_in['wk'], 'L1_gnn_bk': _L1_gnn_in['bk'], 'L1_gnn_wv': _L1_gnn_in['wv'], 'L1_gnn_bv': _L1_gnn_in['bv'], 'L1_gnn_wo': _L1_gnn_in['wo'], 'L1_gnn_bo': _L1_gnn_in['bo'], 'L2_gnn_W': _L2_gnn_in['W'], 'L2_gnn_a': _L2_gnn_in['a'], 'L3_gnn_W': _L3_gnn_in['W'], 'L3_gnn_a': _L3_gnn_in['a']}

def reference(x, adj, L0_gnn_Wq, L0_gnn_bq, L0_gnn_Wk, L0_gnn_bk, L0_gnn_Wv, L0_gnn_bv, L0_gnn_Wo, L0_gnn_bo, L0_gnn_gamma, L0_gnn_beta, L1_gnn_wq, L1_gnn_bq, L1_gnn_wk, L1_gnn_bk, L1_gnn_wv, L1_gnn_bv, L1_gnn_wo, L1_gnn_bo, L2_gnn_W, L2_gnn_a, L3_gnn_W, L3_gnn_a):
    import jax
    import jax.numpy as jnp

    def _L0_gnn_ref(x, adj_matrix, Wq, bq, Wk, bk, Wv, bv, Wo, bo, gamma, beta):
        import jax, jax.numpy as jnp
        import numpy as np
        import math
        CHUNK = 128
        NUM_HEADS = 4
        EPS = 1e-05
        B, N, Fin = x.shape
        H = NUM_HEADS
        Dout = Wq.shape[0]
        Dh = Dout // H
        Nc = N // CHUNK
        q = (x @ Wq.T + bq).reshape(B, N, H, Dh).transpose(0, 2, 1, 3)
        k = (x @ Wk.T + bk).reshape(B, N, H, Dh).transpose(0, 2, 1, 3)
        v = (x @ Wv.T + bv).reshape(B, N, H, Dh).transpose(0, 2, 1, 3)
        kc = k.reshape(B, H, Nc, CHUNK, Dh)
        vc = v.reshape(B, H, Nc, CHUNK, Dh)
        scores = jnp.einsum('bhnd,bhjcd->bhnjc', q, kc) / jnp.sqrt(jnp.asarray(Dh, dtype=q.dtype))
        scores = jnp.clip(scores, -10.0, 10.0)
        mask = adj_matrix.reshape(N, Nc, CHUNK)[None, None]
        scores = jnp.where(mask == 0, jnp.asarray(-10.0, scores.dtype), scores)
        attn = jax.nn.softmax(scores, axis=-1)
        ctx = jnp.einsum('bhnjc,bhjcd->bhnd', attn, vc)
        ctx = ctx.transpose(0, 2, 1, 3).reshape(B, N, Dout)
        out = ctx @ Wo.T + bo
        out = out + x
        mu = jnp.mean(out, axis=-1, keepdims=True)
        var = jnp.mean(jnp.square(out - mu), axis=-1, keepdims=True)
        out = (out - mu) * jax.lax.rsqrt(var + EPS) * gamma + beta
        return out

    def _L1_gnn_ref(x, adj, wq, bq, wk, bk, wv, bv, wo, bo):
        import jax, jax.numpy as jnp
        import numpy as np
        B, N, D_IN, D_OUT, H = (64, 256, 128, 128, 4)
        HD = D_OUT // H
        b, n, _ = x.shape
        q = (x @ wq.T + bq).reshape(b, n, H, HD).transpose(0, 2, 1, 3)
        k = (x @ wk.T + bk).reshape(b, n, H, HD).transpose(0, 2, 1, 3)
        v = (x @ wv.T + bv).reshape(b, n, H, HD).transpose(0, 2, 1, 3)
        scores = jnp.einsum('bhnd,bhmd->bhnm', q, k) / jnp.sqrt(jnp.float32(HD))
        scores = jnp.where(adj[None, None] == 0, -jnp.inf, scores)
        attn = jnp.nan_to_num(jax.nn.softmax(scores, axis=-1), nan=0.0)
        out = jnp.einsum('bhnm,bhmd->bhnd', attn, v)
        out = out.transpose(0, 2, 1, 3).reshape(b, n, D_OUT)
        return out @ wo.T + bo

    def _L2_gnn_ref(h, adj, W, a):
        import jax, jax.numpy as jnp
        import numpy as np
        LEAKY_ALPHA = 0.2
        Fout = W.shape[1]
        Wh = jnp.einsum('bnf,fo->bno', h, W)
        a1 = a[:Fout, 0]
        a2 = a[Fout:, 0]
        s_i = Wh @ a1
        s_j = Wh @ a2
        e = jax.nn.leaky_relu(s_i[:, :, None] + s_j[:, None, :], negative_slope=LEAKY_ALPHA)
        N = Wh.shape[1]
        mask = (adj > 0) | jnp.eye(N, dtype=bool)
        e = jnp.where(mask[None, :, :], e, -jnp.inf)
        attention = jax.nn.softmax(e, axis=-1)
        attention = jnp.nan_to_num(attention, nan=0.0)
        h_prime = jnp.einsum('bij,bjo->bio', attention, Wh)
        return jax.nn.elu(h_prime)

    def _L3_gnn_ref(x, adj, W, a):
        import jax, jax.numpy as jnp
        import numpy as np
        ALPHA = 0.2
        MASK_VAL = -9000000000000000.0
        B, N, _ = x.shape
        H, _, hs = W.shape
        Wh = jnp.einsum('bnf,hfd->bhnd', x, W)
        a1, a2 = (a[:, :hs], a[:, hs:])
        ei = jnp.einsum('bhnd,hd->bhn', Wh, a1)
        ej = jnp.einsum('bhnd,hd->bhn', Wh, a2)
        e = ei[:, :, :, None] + ej[:, :, None, :]
        e = jnp.where(e > 0, e, ALPHA * e)
        e = jnp.where(adj[None, None] > 0, e, MASK_VAL)
        att = jax.nn.softmax(e, axis=-1)
        h = jnp.einsum('bhij,bhjd->bhid', att, Wh)
        h = h.transpose(0, 2, 1, 3).reshape(B, N, H * hs)
        return jax.nn.elu(h)
    x = _layernorm(x + _L0_gnn_ref(x, adj, L0_gnn_Wq, L0_gnn_bq, L0_gnn_Wk, L0_gnn_bk, L0_gnn_Wv, L0_gnn_bv, L0_gnn_Wo, L0_gnn_bo, L0_gnn_gamma, L0_gnn_beta), axis=-1)
    x = _layernorm(x + _L1_gnn_ref(x, adj, L1_gnn_wq, L1_gnn_bq, L1_gnn_wk, L1_gnn_bk, L1_gnn_wv, L1_gnn_bv, L1_gnn_wo, L1_gnn_bo), axis=-1)
    x = _layernorm(x + _L2_gnn_ref(x, adj, L2_gnn_W, L2_gnn_a), axis=-1)
    x = _layernorm(x + _L3_gnn_ref(x, adj, L3_gnn_W, L3_gnn_a), axis=-1)
    return x

_drawn_inputs = setup_inputs


def setup_inputs(seed=0):
    import zlib

    import numpy as np

    out = dict(_drawn_inputs(seed))
    spreads = {'L0_gnn_bq': (0.0, 0.1),
     'L0_gnn_bk': (0.0, 2.0),
     'L0_gnn_bv': (0.0, 0.1),
     'L0_gnn_bo': (0.0, 0.1),
     'L0_gnn_gamma': (1.0, 0.2),
     'L0_gnn_beta': (0.0, 0.1)}
    factors = {'L1_gnn_bq': 8.0, 'L1_gnn_bk': 64.0}
    for name, (base, spread) in spreads.items():
        noise = np.random.default_rng([zlib.crc32(name.encode()), seed]).standard_normal(out[name].shape)
        drawn = base * np.exp(spread * noise) if base else spread * noise
        out[name] = jnp.asarray(drawn.astype(out[name].dtype))
    for name, factor in factors.items():
        out[name] = (out[name] * factor).astype(out[name].dtype)
    return out
```

```python
from contextlib import ExitStack

import concourse.bass as bass
from concourse import mybir

F32 = mybir.dt.float32
F32R = mybir.dt.float32r
BF16 = mybir.dt.bfloat16
F16 = mybir.dt.float16
I32 = mybir.dt.int32
ALU = mybir.AluOpType
ACT = mybir.ActivationFunctionType
AX = mybir.AxisListType

P = 128
GRAPHS, NODES, F = 8, 1024, 128
BLOCKS = NODES // P
HALF = 512
IB = HALF // P
TILES = BLOCKS * 2
LAYERS = 4
HEADS = (4, 4, 1, 4)
WIDTH = tuple(F // h for h in HEADS)
UNITS = tuple(GRAPHS * h for h in HEADS)
UNIT0 = tuple(sum(UNITS[:n]) for n in range(LAYERS))
SHIFT0 = tuple(sum(UNITS[1:n]) for n in range(LAYERS))
BIG = 2.0 ** 100
LEAST = -(2.0 ** 66)
TINY = 2.0 ** -100
EPS = 1e-5
SLOPE = 0.2
SCALE = 32.0 ** -0.5
LN2 = 0.6931471805599453
CLIP_LO = 2.0 * 4.5399929762484854e-05
CLIP_HI = 2.0 * 22026.465794806718
UNROLL = 4
RING = 4
CREDIT = 32
SHIFT_CREDIT = 1
LAG = 3
SHIFT_AT = [k * 3 // 4 for k in range(TILES)]
TURN_AT = 14
V3 = 3 * 33
V3W = 3 * 129
LOADS = (9, 7, 9, 10)
ROWMS = (0, 1, 2, 2)
CHAIN = (4, 19, 13, 20, 8)
HCHAIN = (36, 28, 68, 44)
HPRE = (0, 1, 5, 5)
NODE_LOADS = (1, 5, 5, 2, 5)
NODE_STORES = (6, 6, 7, 8, 1)


def build(nc, t):
    with ExitStack() as ctx:
        def sb(name, shape, dt=F32):
            return ctx.enter_context(nc.sbuf_tensor(name, shape, dt))

        def sem(name):
            return ctx.enter_context(nc.semaphore(name))

        ps = ctx.enter_context(nc.psum_tensor("ps", [P, 8, HALF], F32))
        pf = ps[:, :, :].rearrange("p b n -> p (b n)")

        x_d = nc.dram_tensor("x_d", (GRAPHS, P, BLOCKS, F), F32, kind="Internal").ap()
        ctx_d = nc.dram_tensor("ctx_d", (GRAPHS * 4, P, BLOCKS, 32), F32, kind="Internal").ap()
        ctx2_d = nc.dram_tensor("ctx2_d", (GRAPHS, P, BLOCKS * F), F32, kind="Internal").ap()
        q_d = nc.dram_tensor("q_d", (2, GRAPHS * 4 * 32, NODES), F32, kind="Internal").ap()
        k_d = nc.dram_tensor("k_d", (2, GRAPHS * 4 * 32, NODES), F32, kind="Internal").ap()
        v_d = nc.dram_tensor("v_d", (GRAPHS * 4, P, BLOCKS * V3), BF16, kind="Internal").ap()
        v2_d = nc.dram_tensor("v2_d", (GRAPHS, P, BLOCKS * V3W), BF16, kind="Internal").ap()
        row_d = nc.dram_tensor("row_d", (4, GRAPHS * 8, NODES), F32, kind="Internal").ap()
        col_d = nc.dram_tensor("col_d", (GRAPHS * 8, P, BLOCKS), F32, kind="Internal").ap()
        sum_d = nc.dram_tensor("sum_d", (GRAPHS * 4, P, V3), BF16, kind="Internal").ap()

        ident = sb("ident", [P, P])
        ident_b = sb("ident_b", [P, P], BF16)
        ones_b = sb("ones_b", [P, P], BF16)
        ones_r = sb("ones_r", [P, P], F32R)
        expo = sb("expo", [P, BLOCKS])
        ln2 = sb("ln2", [P, 1])
        anti = sb("anti", [P, P], BF16)
        wts = sb("wts", [P, 10, F])
        rows = sb("rows", [P, 6, F])
        bcol = sb("bcol", [P, 4])
        aa = sb("aa", [P, 2, 8])
        mask_n = sb("mask_n", [P, BLOCKS, NODES], BF16)
        mask_t = sb("mask_t", [P, BLOCKS, NODES], BF16)
        empty = sb("empty", [P, NODES], BF16)

        xr = sb("xr", [P, BLOCKS, F])
        cs = sb("cs", [P, BLOCKS, F])
        work = sb("work", [P, BLOCKS, F])
        tmp = sb("tmp", [P, BLOCKS, F])
        xn = sb("xn", [P, BLOCKS, F])
        cT = sb("cT", [P, NODES])
        xT = sb("xT", [P, NODES])
        stat = sb("stat", [P, 3, BLOCKS])
        full = sb("full", [P, 2, NODES])
        part = sb("part", [P, 2, 2, NODES], F32R)
        rowp = part[0:8, :, :, :].rearrange("p a b n -> p (a b) n")
        vbuf = sb("vbuf", [P, 4, BLOCKS, 3, 33], BF16)
        v2buf = sb("v2buf", [P, BLOCKS, 3, 129], BF16)
        vsum = sb("vsum", [P, F])
        vsumb = sb("vsumb", [P, 4, 3, 33], BF16)
        colp = sb("colp", [P, 8, BLOCKS])
        adj_i = full[:, :, :].bitcast(I32)

        qs = sb("qs", [P, UNROLL, NODES], F32R)
        ks = sb("ks", [P, UNROLL, NODES], F32R)
        vs = sb("vs", [P, UNROLL, BLOCKS * V3W], BF16)
        zs = sb("zs", [P, UNROLL, V3], BF16)
        cols = sb("cols", [P, UNROLL, 2, BLOCKS])
        cols2 = sb("cols2", [P, UNROLL, BLOCKS])
        prob = sb("prob", [P, RING, HALF])
        prob_b = sb("prob_b", [P, RING, HALF])
        phi = sb("phi", [P, RING, HALF], F16)
        plo = sb("plo", [P, RING, HALF], BF16)
        top = sb("top", [P, BLOCKS, 2])
        shift = sb("shift", [P, 3, BLOCKS])
        nshift = sb("nshift", [P, 2, BLOCKS])
        shrow = sb("shrow", [BLOCKS, 2, P], F32R)
        rden = sb("rden", [P, 8])
        blk = work[:, :, :].rearrange("p j (t d) -> p j t d", d=32)
        outp = sb("outp", [P, 2, BLOCKS * F])

        s_const = sem("s_const")
        s_ident = sem("s_ident")
        s_fill = sem("s_fill")
        s_krow = sem("s_krow")
        s_anti = sem("s_anti")
        s_adj = [sem("s_adj_t"), sem("s_adj_n")]
        s_mask = sem("s_mask")
        s_diag = sem("s_diag")
        s_cnt = sem("s_cnt")
        s_empty = sem("s_empty")
        s_load = sem("s_load")
        s_store = sem("s_store")
        s_fin = sem("s_fin")
        s_chain = sem("s_chain")
        s_hchain = sem("s_hchain")
        s_stk = [sem(f"s_stk{n}") for n in range(UNROLL)]
        s_rowm = [sem(f"s_rowm{n}") for n in range(UNROLL)]
        s_cols2 = sem("s_cols2")
        s_score = sem("s_score")
        s_exp = sem("s_exp")
        s_p = sem("s_p")
        s_hi = sem("s_hi")
        s_lo = sem("s_lo")
        s_av = sem("s_av")
        s_accfree = sem("s_accfree")
        s_chfree = sem("s_chfree")
        s_nsc = sem("s_nsc")
        s_nmax = sem("s_nmax")
        s_shcol = sem("s_shcol")
        s_shT = sem("s_shT")
        s_shift = sem("s_shift")
        s_out = sem("s_out")
        s_ctx = sem("s_ctx")
        s_outfree = sem("s_outfree")
        EVENTS = {
            "cT_ps": (1, 2),
            "cT": (1, 2),
            "y_ps": (1, 2),
            "y": (1, 2),
            "eneg": (3, 4),
            "eexp": (3, 4),
            "var": (1, 2, 3, 4),
            "rstd": (1, 2, 3, 4),
            "var0": (1,),
            "rstd0": (1,),
            "xn": (0, 1, 2, 3, 4),
            "xT_ps": (0, 1, 2, 3),
            "xT": (0, 1, 2, 3),
            "q_ps": (0, 1),
            "k_ps": (0, 1),
            "w_ps": (2, 3),
            "v_ps": (0, 1, 2, 3),
            "row_ps": (2, 3),
            "q": (0, 1),
            "k": (0, 1),
            "w": (2, 3),
            "row": (2, 3),
            "col": (2, 3),
            "qk2": (0, 1),
            "row2": (2, 3),
            "vf": (0, 1, 2, 3),
            "v": (0, 1, 2, 3),
        }
        s_ev = {name: sem("s_" + name) for name in EVENTS}

        def ev(name, stage, b):
            assert stage in EVENTS[name]
            return 2 + GRAPHS * EVENTS[name].index(stage) + b

        def before(name, stage, b):
            if stage in EVENTS[name]:
                return 1 + GRAPHS * EVENTS[name].index(stage) + b
            return 1 + GRAPHS * sum(s < stage for s in EVENTS[name])

        def store_at(stage, b):
            return 16 + 16 * GRAPHS * sum(NODE_STORES[:stage]) + b * (16 * NODE_STORES[stage])

        def load_at(stage, b):
            return 16 * GRAPHS * sum(NODE_LOADS[:stage]) + b * (16 * NODE_LOADS[stage])

        def stk_at(layer, n, u):
            return 16 * sum(LOADS[m] * UNITS[m] // UNROLL for m in range(layer)) + (u + 1) * (16 * LOADS[layer])

        def rowm_at(layer, n, u):
            return 16 * sum(ROWMS[m] * UNITS[m] // UNROLL for m in range(layer)) + (u + 1) * (16 * ROWMS[layer])

        def loop(eng, layer, body):
            n = UNITS[layer] // UNROLL
            if n - 1 > 1:
                with eng.Fori(0, n - 1) as u:
                    body(u, False)
            else:
                body(0, False)
            body(n - 1, True)

        x_in = t["x"].rearrange("b (t p) f -> b p t f", p=P)
        x_out = t["out"].rearrange("b (t p) f -> b p t f", p=P)

        def one(ap, i):
            return ap[bass.ds(i, 1)]

        block = ctx.enter_context(nc.Block())

        @block.sync
        def _(sp):
            for k, name in enumerate(("L0_gnn_Wq", "L0_gnn_Wk", "L0_gnn_Wv", "L0_gnn_Wo",
                                      "L1_gnn_wq", "L1_gnn_wk", "L1_gnn_wv", "L1_gnn_wo",
                                      "L2_gnn_W", "L3_gnn_W")):
                sp.dma_start(wts[:, k, :], t[name]).then_inc(s_const, 16)
            for k, name in enumerate(("L0_gnn_bv", "L0_gnn_bo", "L1_gnn_bv", "L1_gnn_bo",
                                      "L0_gnn_gamma", "L0_gnn_beta")):
                sp.dma_start(rows[:, k, :], t[name]).then_inc(s_const, 16)
            for k, name in enumerate(("L0_gnn_bq", "L0_gnn_bk", "L1_gnn_bq", "L1_gnn_bk")):
                sp.dma_start(bcol[:, k:k + 1], t[name]).then_inc(s_const, 16)
            sp.dma_start(aa[:, 0, 0:2], t["L2_gnn_a"]).then_inc(s_const, 16)
            sp.dma_start(aa[:, 1, :], t["L3_gnn_a"]).then_inc(s_const, 16)

            def adjacency(layer):
                for k in range(2 * BLOCKS):
                    src = t["adj_n" if k % 2 else "adj_t"]
                    sp.wait_ge(s_mask, CREDIT + 16 * layer + k - 1)
                    sp.dma_start(adj_i[:, k % 2, :], src[k // 2 * P:(k // 2 + 1) * P, :]).then_inc(s_adj[k % 2], 16)
                sp.wait_ge(s_mask, CREDIT + 16 * (layer + 1))

            def node(stage):
                with sp.Fori(0, GRAPHS) as b:
                    sp.wait_ge(s_ev["xn"], before("xn", stage, b))
                    if stage == 0:
                        sp.wait_ge(s_store, store_at(stage, b))
                        src = one(x_in, b)
                    else:
                        src = one(x_d, b)
                    dst = xn if stage == 0 else xr
                    if stage == 0:
                        sp.wait_ge(s_ev["xT_ps"], before("xT_ps", stage, b))
                    sp.dma_start(dst[:, :, :], src.rearrange("a p t f -> (a p) t f")).then_inc(s_load, 16)
                    if stage in (1, 2, 4):
                        for h in range(4):
                            sp.dma_start(cs[:, :, 32 * h:32 * h + 32],
                                         one(ctx_d, b * 4 + h).rearrange("a p t f -> (a p) t f")
                                         ).then_inc(s_load, 16)
                    if stage == 3:
                        sp.dma_start(cs[:, :, :].rearrange("p t f -> p (t f)"),
                                     one(ctx2_d, b).rearrange("a p n -> (a p) n")).then_inc(s_load, 16)
                    sp.wait_ge(s_ev["xn"], ev("xn", stage, b))
                    dst = x_out if stage == 4 else x_d
                    sp.dma_start(one(dst, b).rearrange("a p t f -> (a p) t f"), xn[:, :, :]
                                 ).then_inc(s_store, 16)
                    if stage in (0, 1):
                        sp.wait_ge(s_ev["qk2"], ev("qk2", stage, b))
                        for w, dst in enumerate((q_d, k_d)):
                            for s in range(2):
                                sp.dma_start(dst[s, bass.ds(b * P, P)], part[:, w, s, :].bitcast(F32)
                                             ).then_inc(s_store, 16)
                        sp.wait_ge(s_ev["v"], ev("v", stage, b))
                        sp.dma_start(v_d[bass.ds(b * 4, 4)].rearrange("h p n -> p h n"),
                                     vbuf[:, :, :, :, :].rearrange("p h t s d -> p h (t s d)")
                                     ).then_inc(s_store, 16)
                    if stage in (2, 3):
                        n = 2 * HEADS[stage]
                        sp.wait_ge(s_ev["row2"], ev("row2", stage, b))
                        for kind in range(4):
                            sp.dma_start(row_d[kind, bass.ds(b * 8, n)], rowp[0:n, kind, :].bitcast(F32)
                                         ).then_inc(s_store, 16)
                        sp.dma_start(col_d[bass.ds(b * 8, n)].rearrange("r p t -> p r t"), colp[:, 0:n, :]
                                     ).then_inc(s_store, 16)
                        sp.wait_ge(s_ev["v"], ev("v", stage, b))
                        if stage == 2:
                            sp.dma_start(one(v2_d, b).rearrange("a p n -> (a p) n"),
                                         v2buf[:, :, :, :].rearrange("p t s d -> p (t s d)")
                                         ).then_inc(s_store, 16)
                        else:
                            sp.dma_start(v_d[bass.ds(b * 4, 4)].rearrange("h p n -> p h n"),
                                         vbuf[:, :, :, :, :].rearrange("p h t s d -> p h (t s d)")
                                         ).then_inc(s_store, 16)
                            sp.dma_start(sum_d[bass.ds(b * 4, 4)].rearrange("h p n -> p h n"),
                                         vsumb[:, :, :, :].rearrange("p h s d -> p h (s d)")
                                         ).then_inc(s_store, 16)

            def load_unit(layer, u, m):
                g, n = u * UNROLL + m, m % UNROLL
                count = 0

                def go(dst, src):
                    nonlocal count
                    count += 1
                    sp.dma_start(dst, src).then_inc(s_stk[n], 16)

                if layer < 2:
                    for r, (a, c) in enumerate(((0, 0), (0, 1), (1, 0), (1, 1))[:4 - layer]):
                        go(qs[32 * r:32 * r + 32, n, :].bitcast(F32), q_d[a, bass.ds(g * 32, 32)])
                        go(ks[32 * r:32 * r + 32, n, :].bitcast(F32), k_d[c, bass.ds(g * 32, 32)])
                    go(vs[:, n, 0:BLOCKS * V3], one(v_d, g).rearrange("a p n -> (a p) n"))
                else:
                    heads = HEADS[layer]
                    r = g * 8 if heads == 1 else (u + m // UNROLL) * 8 + n
                    for k in range(2):
                        go(qs[k:k + 1, n, :].bitcast(F32), row_d[k, bass.ds(r, 1)])
                        go(ks[k:k + 1, n, :].bitcast(F32), row_d[2 + k, bass.ds(r, 1)])
                        go(ks[32 + k:33 + k, n, :].bitcast(F32), row_d[k, bass.ds(r + heads, 1)])
                    for k in range(2):
                        go(cols[:, n, k, :], one(col_d, r + k * heads).rearrange("a p t -> (a p) t"))
                    if layer == 2:
                        go(vs[:, n, :], one(v2_d, g).rearrange("a p n -> (a p) n"))
                    else:
                        go(vs[:, n, 0:BLOCKS * V3], one(v_d, g).rearrange("a p n -> (a p) n"))
                        go(zs[:, n, :], one(sum_d, g).rearrange("a p n -> (a p) n"))
                assert count == LOADS[layer]

            def place_shift(layer, g, n):
                sp.wait_ge(s_shift, SHIFT_CREDIT + SHIFT0[layer] + g + 1)
                for dst in ((qs[96:97, n, :],) if layer == 1 else (qs[2:3, n, :], ks[2:3, n, :])):
                    sp.dma_start(dst.bitcast(F32).rearrange("a (t p) -> a t p", p=P),
                                 shrow[:, n % 2, :].bitcast(F32)).then_inc(s_rowm[n], 16)

            def heads(layer):
                sp.wait_ge(s_store, store_at(layer, GRAPHS))
                for n in range(2):
                    load_unit(layer, 0, n)
                if layer:
                    place_shift(layer, 0, 0)

                def body(u, last):
                    for n in range(UNROLL):
                        g = u * UNROLL + n
                        if not (last and n >= UNROLL - 2):
                            sp.wait_ge(s_av, CREDIT + TILES * (UNIT0[layer] - 1) + g * TILES)
                            load_unit(layer, u, n + 2)
                        if layer and not (last and n == UNROLL - 1):
                            place_shift(layer, g + 1, (n + 1) % UNROLL)

                loop(sp, layer, body)
                sp.wait_ge(s_outfree, CREDIT + UNIT0[layer] + UNITS[layer])

            adjacency(0)
            node(0)
            heads(0)
            adjacency(1)
            node(1)
            heads(1)
            adjacency(2)
            node(2)
            heads(2)
            adjacency(3)
            node(3)
            heads(3)
            node(4)
            sp.wait_ge(s_store, store_at(4, GRAPHS))

        @block.gpsimd
        def _(pool):
            pool.memset(ident[:, :], 0.0).then_inc(s_ident, 1)
            pool.memset(ident_b[:, :], 0.0).then_inc(s_ident, 1)
            pool.memset(expo[:, :], -0.5).then_inc(s_ident, 1)
            pool.wait_ge(s_ident, 3)
            for m in (ident, ident_b):
                pool.affine_select(out=m[:, :], in_=m[:, :], compare_op=ALU.not_equal, fill=1.0, base=0,
                                   pattern=[[-1, P]], channel_multiplier=1).then_inc(s_ident, 1)
            pool.memset(anti[:, :], 1.0).then_inc(s_anti, 1)
            pool.wait_ge(s_anti, 1)
            pool.affine_select(out=anti[:, :], in_=anti[:, :], compare_op=ALU.not_equal, fill=0.0, base=0,
                               pattern=[[-1, P]], channel_multiplier=1).then_inc(s_anti, 1)
            pool.sem_inc(s_outfree, CREDIT)
            pool.sem_inc(s_store, 16)
            for name in ("rstd", "rstd0"):
                pool.sem_inc(s_ev[name], 1)

            def node(stage):
                with pool.Fori(0, GRAPHS) as b:
                    for name in (("0",) if stage == 1 else ()) + ("",):
                        pool.wait_ge(s_ev["var" + name], ev("var" + name, stage, b))
                        pool.tensor_tensor(stat[:, 2, :], stat[:, 1, :], expo[:, :], ALU.pow
                                           ).then_inc(s_ev["rstd" + name], 1)

            def heads(layer):
                def body(u, last):
                    for n in range(UNROLL):
                        g = u * UNROLL + n
                        pool.wait_ge(s_out, UNIT0[layer] + g + 1)
                        if layer == 2:
                            pool.dma_start(one(ctx2_d, g).rearrange("a p n -> (a p) n"), outp[:, n % 2, :]
                                           ).then_inc(s_ctx, 16)
                        else:
                            pool.dma_start(one(ctx_d, g).rearrange("a p t f -> (a p) (t f)"),
                                           outp[:, n % 2, 0:BLOCKS * 32]).then_inc(s_ctx, 16)
                        pool.wait_ge(s_ctx, 16 * (UNIT0[layer] + 1) + g * 16)
                        pool.sem_inc(s_outfree, 1)

                loop(pool, layer, body)

            heads(0)
            node(1)
            heads(1)
            node(2)
            heads(2)
            node(3)
            heads(3)
            node(4)

        @block.scalar
        def _(act):
            for name in ("cT", "eexp", "xT", "q", "k", "w", "row"):
                act.sem_inc(s_ev[name], 1)
            act.sem_inc(s_exp, CREDIT)
            act.sem_inc(s_hi, CREDIT)
            act.wait_ge(s_const, 16 * 22)

            def node(stage):
                with act.Fori(0, GRAPHS) as b:
                    if stage in (1, 2):
                        act.wait_ge(s_ev["cT_ps"], ev("cT_ps", stage, b))
                        act.wait_ge(s_ev["y_ps"], before("y_ps", stage, b))
                        act.activation(cT[:, :], pf[:, 0:NODES], ACT.Copy).then_inc(s_ev["cT"], 1)
                    if stage in (3, 4):
                        act.wait_ge(s_ev["eneg"], ev("eneg", stage, b))
                        act.activation(tmp[:, :, :], tmp[:, :, :], ACT.Exp).then_inc(s_ev["eexp"], 1)
                    if stage < 4:
                        act.wait_ge(s_ev["xT_ps"], ev("xT_ps", stage, b))
                        act.wait_ge(s_ev["v_ps"], before("v_ps", stage, b))
                        act.activation(xT[:, :], pf[:, 0:NODES], ACT.Copy).then_inc(s_ev["xT"], 1)
                    if stage < 2:
                        for w, name in enumerate("qk"):
                            act.wait_ge(s_ev[name + "_ps"], ev(name + "_ps", stage, b))
                            act.wait_ge(s_ev["qk2"], before("qk2", stage, b))
                            act.activation(full[:, w, :], pf[:, (4 + 2 * w) * HALF:(6 + 2 * w) * HALF], ACT.Identity,
                                           bias=bcol[:, 2 * stage + w:2 * stage + w + 1]).then_inc(s_ev[name], 1)
                    elif stage < 4:
                        n = 2 * HEADS[stage]
                        act.wait_ge(s_ev["w_ps"], ev("w_ps", stage, b))
                        act.wait_ge(s_ev["row_ps"], before("row_ps", stage, b))
                        act.activation(full[:, 0, :], pf[:, 4 * HALF:6 * HALF], ACT.Copy).then_inc(s_ev["w"], 1)
                        act.wait_ge(s_ev["row_ps"], ev("row_ps", stage, b))
                        act.wait_ge(s_ev["row2"], before("row2", stage, b))
                        act.activation(full[0:n, 1, :], pf[0:n, 6 * HALF:8 * HALF], ACT.Copy
                                       ).then_inc(s_ev["row"], 1)

            def heads(layer):
                def body(u, last):
                    def tile_value(s):
                        return CREDIT + TILES * UNIT0[layer] + u * (TILES * UNROLL) + s

                    def exps(s):
                        n, j, r = s // TILES, s % BLOCKS, s % RING
                        T = tile_value(s)
                        act.wait_ge(s_score, T - CREDIT + 1)
                        act.wait_ge(s_lo, T - RING + 1)
                        if layer == 0:
                            act.activation(prob[:, r, :], ps[:, r, :], ACT.Exp, scale=SCALE, bias=ln2[:, 0:1]
                                           ).then_inc(s_exp, 1)
                        elif layer == 1:
                            act.activation(prob[:, r, :], ps[:, r, :], ACT.Exp, scale=SCALE).then_inc(s_exp, 1)
                            act.wait_ge(s_av, T - RING + 1)
                            act.activation(phi[:, r, :], ps[:, r, :], ACT.Exp, scale=SCALE).then_inc(s_hi, 1)
                        else:
                            y = 2 * (s % 2)
                            if j == 0:
                                act.wait_ge(s_cols2, UNIT0[layer] - UNIT0[2] + u * UNROLL + n + 1)
                            act.activation(prob[:, r, :], ps[:, y, :], ACT.Exp, bias=cols[:, n, 1, j:j + 1])
                            act.activation(prob_b[:, r, :], ps[:, y + 1, :], ACT.Exp, bias=cols2[:, n, j:j + 1]
                                           ).then_inc(s_exp, 1)

                    def high(s):
                        T, r = tile_value(s), s % RING
                        act.wait_ge(s_p, T - CREDIT + 1 - (TILES * UNITS[1] if layer > 1 else 0))
                        act.wait_ge(s_av, T - RING + 1)
                        act.activation(phi[:, r, :], prob[:, r, :], ACT.Copy).then_inc(s_hi, 1)

                    for s in range(TILES * UNROLL + 1):
                        if s < TILES * UNROLL:
                            exps(s)
                        if s and layer != 1:
                            high(s - 1)

                loop(act, layer, body)

            act.wait_ge(s_fill, 9)
            node(0)
            heads(0)
            node(1)
            heads(1)
            node(2)
            heads(2)
            node(3)
            heads(3)
            node(4)

        @block.tensor
        def _(pe):
            for name in ("cT_ps", "y_ps", "xT_ps", "q_ps", "k_ps", "w_ps", "v_ps", "row_ps"):
                pe.sem_inc(s_ev[name], 1)
            pe.sem_inc(s_av, CREDIT)
            pe.wait_ge(s_const, 16 * 22)
            pe.wait_ge(s_ident, 5)
            pe.wait_ge(s_fill, 9)

            def node(stage):
                with pe.Fori(0, GRAPHS) as b:
                    if stage in (1, 2):
                        wo = wts[:, 4 * (stage - 1) + 3, :]
                        pe.wait_ge(s_load, load_at(stage, b + 1))
                        if stage == 2:
                            pe.wait_ge(s_ev["col"], before("col", stage, b))
                        for it in range(BLOCKS):
                            mm = pe.transpose(pf[:, it * P:(it + 1) * P], cs[:, it, :], ident[:, :])
                        mm.then_inc(s_ev["cT_ps"], 1)
                        pe.wait_ge(s_ev["cT"], ev("cT", stage, b))
                        pe.wait_ge(s_ev["vf"], before("vf", stage, b))
                        for it in range(BLOCKS):
                            mm = pe.matmul(pf[:, 2 * HALF + it * P:2 * HALF + (it + 1) * P],
                                           cT[:, it * P:(it + 1) * P], wo, start=True, stop=True)
                        mm.then_inc(s_ev["y_ps"], 1)
                    if stage == 4:
                        return
                    if stage == 0:
                        pe.wait_ge(s_load, load_at(stage, b + 1))
                    else:
                        pe.wait_ge(s_ev["xn"], ev("xn", stage, b))
                    if stage == 3 or stage == 2:
                        pe.wait_ge(s_ev["col"], before("col", stage, b))
                    for it in range(BLOCKS):
                        mm = pe.transpose(pf[:, it * P:(it + 1) * P], xn[:, it, :], ident[:, :])
                    mm.then_inc(s_ev["xT_ps"], 1)
                    pe.wait_ge(s_ev["xT"], ev("xT", stage, b))
                    if stage < 2:
                        for w, name in enumerate("qk"):
                            pe.wait_ge(s_ev[name], before(name, stage, b))
                            for c in range(2):
                                mm = pe.matmul(ps[:, 4 + 2 * w + c, :], wts[:, 4 * stage + w, :],
                                               xT[:, c * HALF:(c + 1) * HALF], start=True, stop=True)
                            mm.then_inc(s_ev[name + "_ps"], 1)
                        wv = wts[:, 4 * stage + 2, :]
                    else:
                        n, wv = 2 * HEADS[stage], wts[:, 6 + stage, :]
                        pe.wait_ge(s_ev["w"], before("w", stage, b))
                        for c in range(2):
                            mm = pe.matmul(ps[:, 4 + c, :], wv, xT[:, c * HALF:(c + 1) * HALF],
                                           start=True, stop=True)
                        mm.then_inc(s_ev["w_ps"], 1)
                    pe.wait_ge(s_ev["vf"], before("vf", stage, b))
                    if stage in (1, 2):
                        pe.wait_ge(s_ev["y"], ev("y", stage, b))
                    for it in range(BLOCKS):
                        mm = pe.matmul(pf[:, 2 * HALF + it * P:2 * HALF + (it + 1) * P],
                                       xT[:, it * P:(it + 1) * P], wv, start=True, stop=True)
                    mm.then_inc(s_ev["v_ps"], 1)
                    if stage >= 2:
                        a = aa[:, stage - 2, 0:n]
                        pe.wait_ge(s_ev["w"], ev("w", stage, b))
                        pe.wait_ge(s_ev["row"], before("row", stage, b))
                        for c in range(2):
                            pe.matmul(ps[0:n, 6 + c, :], a, full[:, 0, c * HALF:(c + 1) * HALF],
                                      start=True, stop=True)
                        for it in range(BLOCKS):
                            mm = pe.matmul(ps[:, 0, it * n:(it + 1) * n], full[:, 0, it * P:(it + 1) * P], a,
                                           start=True, stop=True)
                        mm.then_inc(s_ev["row_ps"], 1)

            def heads(layer):
                width = WIDTH[layer] + 1

                def unit_ready(n, u):
                    pe.wait_ge(s_stk[n], stk_at(layer, n, u))

                def top_scores(n, k, U):
                    it, c = k // 2, k % 2
                    bank = ps[:, 4 + k % 2, :]
                    pe.wait_ge(s_nmax, CREDIT + TILES * U + k - 1)
                    if k == 0:
                        pe.wait_ge(s_shift, SHIFT_CREDIT + U)
                    cut = slice(c * HALF, (c + 1) * HALF)
                    pe.matmul(bank, ident_b[:, :], mask_n[:, it, cut], start=True, stop=False)
                    if layer == 1:
                        mm = pe.matmul(bank, qs[0:96, n, it * P:(it + 1) * P], ks[0:96, n, cut],
                                       start=False, stop=True)
                    else:
                        mm = pe.matmul(bank, ones_r[32:34, :], ks[32:34, n, cut], start=False, stop=True,
                                       tile_position=(32, 0))
                    mm.then_inc(s_nsc, 1)

                def turn_shift(n, U):
                    pe.wait_ge(s_shcol, U + 1)
                    pe.transpose(ps[0:BLOCKS, 4, 0:P], nshift[:, n % 2, :], ident[:, :]).then_inc(s_shT, 1)

                def body(u, last):
                    def tile_value(s):
                        return CREDIT + TILES * UNIT0[layer] + u * (TILES * UNROLL) + s

                    def scores(s):
                        n, tt = s // TILES, s % TILES
                        c, j = tt // BLOCKS, tt % BLOCKS
                        cut, blk_j = slice(c * HALF, (c + 1) * HALF), slice(j * P, (j + 1) * P)
                        T = tile_value(s)
                        if tt == 0:
                            unit_ready(n, u)
                            if layer:
                                pe.wait_ge(s_rowm[n], rowm_at(layer, n, u))
                        if layer < 2:
                            bank = ps[:, s % RING, :]
                            pe.wait_ge(s_exp if layer == 0 else s_hi, T - RING + 1)
                            pe.matmul(bank, ident_b[:, :], mask_t[:, j, cut], start=True, stop=False)
                            depth = 128 if layer == 0 else 97
                            mm = pe.matmul(bank, ks[0:depth, n, blk_j], qs[0:depth, n, cut],
                                           start=False, stop=True)
                        else:
                            pe.wait_ge(s_exp, T - 1)
                            for k, rows_of in enumerate((qs, ks)):
                                bank = ps[:, 2 * (s % 2) + k, :]
                                pe.matmul(bank, ident_b[:, :], mask_t[:, j, cut], start=True, stop=False)
                                mm = pe.matmul(bank, ones_r[0:3, :], rows_of[0:3, n, cut],
                                               start=False, stop=True)
                        mm.then_inc(s_score, 1)

                    def weigh(s):
                        n, tt, r = s // TILES, s % TILES, s % RING
                        c, j = tt // BLOCKS, tt % BLOCKS
                        H = CREDIT + 2 * UNIT0[layer] + u * (2 * UNROLL) + 2 * n + c
                        T = tile_value(s)
                        if layer == 0:
                            if j % 2 == 0:
                                pe.wait_ge(s_chfree, CREDIT + u * (TILES // 2 * UNROLL) + s // 2 - 1)
                        elif j == 0:
                            pe.wait_ge(s_accfree, H - (0 if layer == 2 else 1) - 2 * UNITS[0])
                        pe.wait_ge(s_hi, T + 1)
                        pe.wait_ge(s_lo, T + 1)
                        for it in range(IB):
                            if layer == 0:
                                acc = ps[:, 6 + s // 2 % 2, (s % 2 * IB + it) * 33:(s % 2 * IB + it + 1) * 33]
                                opens = s % 2 == 0 and it == 0
                            elif layer == 2:
                                acc = ps[:, 6 + it // 2, it % 2 * width:(it % 2 + 1) * width]
                                opens = j == 0 and it % 2 == 0
                            else:
                                acc = ps[:, 6 + c, it * width:(it + 1) * width]
                                opens = j == 0 and it == 0
                            for h, half in enumerate((phi, plo)):
                                for v in range(3):
                                    at = (j * 3 + v) * width
                                    mm = pe.matmul(acc, half[:, r, it * P:(it + 1) * P], vs[:, n, at:at + width],
                                                   start=opens and h == 0 and v == 0, stop=h == 1 and v == 2,
                                                   skip_group_check=True)
                            if layer == 3 and j == BLOCKS - 1:
                                at_i = c * HALF + it * P
                                for v in range(3):
                                    mm = pe.matmul(acc, empty[:, at_i:at_i + P], zs[:, n, v * 33:(v + 1) * 33],
                                                   start=False, stop=v == 2, skip_group_check=True)
                        mm.then_inc(s_av, 1)

                    for s in range(TILES * UNROLL + LAG):
                        if s < TILES * UNROLL:
                            scores(s)
                            n = s // TILES
                            if layer and not (last and n == UNROLL - 1):
                                for k in range(TILES):
                                    if SHIFT_AT[k] == s % TILES:
                                        if k == 0:
                                            unit_ready((n + 1) % UNROLL, u + (n + 1) // UNROLL)
                                        top_scores((n + 1) % UNROLL, k, SHIFT0[layer] + u * UNROLL + n + 1)
                                if s % TILES == TURN_AT:
                                    turn_shift((n + 1) % UNROLL, SHIFT0[layer] + u * UNROLL + n + 1)
                        if s >= LAG:
                            weigh(s - LAG)

                if layer:
                    unit_ready(0, 0)
                    for k in range(TILES):
                        top_scores(0, k, SHIFT0[layer])
                    turn_shift(0, SHIFT0[layer])
                loop(pe, layer, body)

            node(0)
            pe.wait_ge(s_mask, CREDIT + 16)
            heads(0)
            node(1)
            pe.wait_ge(s_mask, CREDIT + 32)
            pe.wait_ge(s_krow, 1)
            heads(1)
            node(2)
            pe.wait_ge(s_mask, CREDIT + 48)
            pe.wait_ge(s_diag, 16)
            heads(2)
            node(3)
            pe.wait_ge(s_mask, CREDIT + 64)
            for c in range(2):
                for j in range(BLOCKS):
                    mm = pe.matmul(ps[:, 4 + c, :], ones_b[:, :], mask_t[:, j, c * HALF:(c + 1) * HALF],
                                   start=j == 0, stop=j == BLOCKS - 1)
            mm.then_inc(s_cnt, 1)
            pe.wait_ge(s_empty, 1)
            heads(3)

        @block.vector
        def _(dve):
            for name in ("y", "eneg", "var", "var0", "xn", "col", "qk2", "row2", "vf", "v"):
                dve.sem_inc(s_ev[name], 1)
            dve.sem_inc(s_shift, SHIFT_CREDIT)
            for s in (s_mask, s_lo, s_nmax, s_accfree, s_chfree):
                dve.sem_inc(s, CREDIT)
            dve.memset(ones_b[:, :], 1.0).then_inc(s_fill, 1)
            dve.memset(ones_r[:, :].bitcast(F32), 1.0).then_inc(s_fill, 1)
            dve.memset(ln2[:, :], LN2).then_inc(s_fill, 1)
            dve.memset(vbuf[:, :, :, :, :], 0.0).then_inc(s_fill, 1)
            dve.memset(v2buf[:, :, :, :], 0.0).then_inc(s_fill, 1)
            dve.memset(vsumb[:, :, :, :], 0.0).then_inc(s_fill, 1)
            dve.wait_ge(s_fill, 6)
            dve.memset(vbuf[:, :, :, 0, 32], 1.0).then_inc(s_fill, 1)
            dve.memset(v2buf[:, :, 0, 128], 1.0).then_inc(s_fill, 1)
            dve.memset(vsumb[:, :, 0, 32], float(BLOCKS)).then_inc(s_fill, 1)
            dve.wait_ge(s_fill, 9)
            dve.wait_ge(s_ident, 5)
            dve.wait_ge(s_anti, 2)
            dve.wait_ge(s_const, 16 * 22)

            def masks(layer):
                for k in range(2 * BLOCKS):
                    dve.wait_ge(s_adj[k % 2], 16 * (BLOCKS * layer + k // 2 + 1))
                    dst = (mask_n if k % 2 else mask_t)[:, k // 2, :]
                    dve.tensor_scalar(dst, adj_i[:, k % 2, :], 0.0, -BIG, ALU.is_equal if layer < 2 else ALU.is_le,
                                      ALU.mult).then_inc(s_mask, 1)
                    if layer == 2:
                        dve.wait_ge(s_mask, CREDIT + 16 * layer + k + 1)
                        d = dst[:, k // 2 * P:(k // 2 + 1) * P]
                        dve.tensor_tensor(d, d, anti[:, :], ALU.mult).then_inc(s_diag, 1)

            def node(stage):
                chain0 = GRAPHS * sum(CHAIN[:stage])
                with dve.Fori(0, GRAPHS) as b:
                    n_chain = 0

                    def link(ins):
                        nonlocal n_chain
                        n_chain += 1
                        ins.then_inc(s_chain, 1)
                        dve.wait_ge(s_chain, chain0 + b * CHAIN[stage] + n_chain)

                    def wide(ap):
                        return ap.unsqueeze(2).to_broadcast([P, BLOCKS, F])

                    def row(k):
                        return rows[:, k, :].unsqueeze(1).to_broadcast([P, BLOCKS, F])

                    def signal(name, ins):
                        ins.then_inc(s_ev[name], 1)

                    def layer_norm(dst, name):
                        link(dve.tensor_reduce(stat[:, 0, :], work[:, :, :], AX.X, ALU.add))
                        link(dve.tensor_scalar(stat[:, 0, :], stat[:, 0, :], 1.0 / F, None, ALU.mult))
                        link(dve.tensor_tensor(work[:, :, :], work[:, :, :], wide(stat[:, 0, :]), ALU.subtract))
                        link(dve.tensor_tensor(tmp[:, :, :], work[:, :, :], work[:, :, :], ALU.mult))
                        link(dve.tensor_reduce(stat[:, 1, :], tmp[:, :, :], AX.X, ALU.add))
                        dve.tensor_scalar(stat[:, 1, :], stat[:, 1, :], 1.0 / F, EPS, ALU.mult, ALU.add
                                          ).then_inc(s_ev["var" + name], 1)
                        dve.wait_ge(s_ev["rstd" + name], ev("rstd" + name, stage, b))
                        return dve.tensor_tensor(dst, work[:, :, :], wide(stat[:, 2, :]), ALU.mult)

                    if stage in (1, 2):
                        dve.wait_ge(s_load, load_at(stage, b + 1))
                        dve.wait_ge(s_ev["y_ps"], ev("y_ps", stage, b))
                        y = pf[:, 2 * HALF:4 * HALF].rearrange("p (t f) -> p t f", f=F)
                        dve.tensor_tensor(work[:, :, :], y, row(2 * stage - 1), ALU.add).then_inc(s_ev["y"], 1)
                        dve.wait_ge(s_ev["y"], ev("y", stage, b))
                        link(dve.tensor_tensor(work[:, :, :], work[:, :, :], xr[:, :, :], ALU.add))
                    if stage == 1:
                        link(layer_norm(work[:, :, :], "0"))
                        link(dve.tensor_tensor(work[:, :, :], work[:, :, :], row(4), ALU.mult))
                        link(dve.tensor_tensor(work[:, :, :], work[:, :, :], row(5), ALU.add))
                        link(dve.tensor_tensor(work[:, :, :], work[:, :, :], xr[:, :, :], ALU.add))
                    if stage in (3, 4):
                        dve.wait_ge(s_load, load_at(stage, b + 1))
                        dve.tensor_scalar(tmp[:, :, :], cs[:, :, :], 0.0, None, ALU.min).then_inc(s_ev["eneg"], 1)
                        dve.wait_ge(s_ev["eexp"], ev("eexp", stage, b))
                        link(dve.tensor_scalar(tmp[:, :, :], tmp[:, :, :], -1.0, None, ALU.add))
                        link(dve.scalar_tensor_tensor(work[:, :, :], cs[:, :, :], 0.0, tmp[:, :, :],
                                                      ALU.max, ALU.add))
                        link(dve.tensor_tensor(work[:, :, :], work[:, :, :], xr[:, :, :], ALU.add))
                    if stage:
                        dve.wait_ge(s_store, store_at(stage, b))
                        signal("xn", layer_norm(xn[:, :, :], ""))
                        dve.wait_ge(s_ev["xn"], ev("xn", stage, b))
                    else:
                        dve.wait_ge(s_load, load_at(stage, b + 1))
                        dve.sem_inc(s_ev["xn"], 1)
                    if stage == 4:
                        assert n_chain == CHAIN[stage], (stage, n_chain)
                        return
                    dve.wait_ge(s_store, store_at(stage, b))
                    if stage < 2:
                        dve.wait_ge(s_ev["q"], ev("q", stage, b))
                        dve.wait_ge(s_ev["k"], ev("k", stage, b))
                        link(dve.tensor_copy(part[:, :, 0, :], full[:, :, :]))
                        signal("qk2", dve.tensor_tensor(part[:, :, 1, :], full[:, :, :],
                                                        part[:, :, 0, :].bitcast(F32), ALU.subtract))
                    else:
                        n = 2 * HEADS[stage]
                        dve.wait_ge(s_ev["row"], ev("row", stage, b))
                        signal("col", dve.tensor_copy(colp[:, 0:n, :],
                                                      ps[:, 0, 0:BLOCKS * n].rearrange("p (t r) -> p r t", r=n)))
                        r = full[0:n, 1, :]
                        link(dve.tensor_copy(rowp[0:n, 0, :], r))
                        link(dve.tensor_tensor(rowp[0:n, 1, :], r, rowp[0:n, 0, :].bitcast(F32), ALU.subtract))
                        link(dve.tensor_scalar(r, r, SLOPE, None, ALU.mult))
                        link(dve.tensor_copy(rowp[0:n, 2, :], r))
                        dve.wait_ge(s_ev["col"], ev("col", stage, b))
                        signal("row2", dve.tensor_tensor(rowp[0:n, 3, :], r, rowp[0:n, 2, :].bitcast(F32),
                                                         ALU.subtract))
                    dve.wait_ge(s_ev["v_ps"], ev("v_ps", stage, b))
                    v = pf[:, 2 * HALF:4 * HALF].rearrange("p (t f) -> p t f", f=F)
                    if stage < 2:
                        signal("vf", dve.tensor_tensor(tmp[:, :, :], v, row(2 * stage), ALU.add))
                    else:
                        signal("vf", dve.tensor_copy(tmp[:, :, :], v))
                    dve.wait_ge(s_ev["vf"], ev("vf", stage, b))
                    if stage == 3:
                        link(dve.tensor_reduce(vsum[:, :], tmp[:, :, :].rearrange("p t f -> p f t"), AX.X, ALU.add))
                        z, zf = (lambda s: vsumb[:, :, s, 0:32]), vsum[:, :].rearrange("p (h d) -> p h d", h=4)
                        link(dve.tensor_copy(z(0), zf))
                        link(dve.tensor_tensor(zf, zf, z(0), ALU.subtract))
                        link(dve.tensor_copy(z(1), zf))
                        link(dve.tensor_tensor(z(2), zf, z(1), ALU.subtract))
                    if stage == 2:
                        cut, f = (lambda s: v2buf[:, :, s, 0:F]), tmp[:, :, :]
                    else:
                        cut = lambda s: vbuf[:, :, :, s, 0:32]
                        f = tmp[:, :, :].rearrange("p t (h d) -> p h t d", h=4)
                    link(dve.tensor_copy(cut(0), f))
                    link(dve.tensor_tensor(f, f, cut(0), ALU.subtract))
                    link(dve.tensor_copy(cut(1), f))
                    signal("v", dve.tensor_tensor(cut(2), f, cut(1), ALU.subtract))
                    dve.wait_ge(s_ev["v"], ev("v", stage, b))
                    assert n_chain == CHAIN[stage], (stage, n_chain)

            def heads(layer):
                width = WIDTH[layer]
                per = HCHAIN[layer]
                chain0 = sum(HCHAIN[m] * UNITS[m] // UNROLL for m in range(layer))
                state = {}

                def link(ins):
                    state["n"] += 1
                    ins.then_inc(s_hchain, 1)
                    dve.wait_ge(s_hchain, state["base"] + state["n"])

                def find_shift(n):
                    M, z, l = shift[:, 0, :], shift[:, 1, :], shift[:, 2, :]
                    link(dve.tensor_reduce(M, top[:, :, :], AX.X, ALU.max))
                    if layer == 1:
                        dve.tensor_scalar(nshift[:, n % 2, :], M, LEAST, -1.0, ALU.max, ALU.mult
                                          ).then_inc(s_shcol, 1)
                    else:
                        link(dve.tensor_tensor(z, M, cols[:, n, 0, :], ALU.add))
                        link(dve.tensor_scalar(z, z, LEAST, None, ALU.max))
                        link(dve.tensor_scalar(l, z, SLOPE, None, ALU.mult))
                        link(dve.tensor_tensor(l, z, l, ALU.max))
                        dve.tensor_scalar(nshift[:, n % 2, :], l, -1.0, None, ALU.mult).then_inc(s_shcol, 1)
                        dve.tensor_scalar(cols2[:, n, :], cols[:, n, 1, :], SLOPE, None, ALU.mult
                                          ).then_inc(s_cols2, 1)

                def shift_rows(n, U):
                    dve.wait_ge(s_shT, U + 1)
                    dve.tensor_copy(shrow[:, n % 2, :], ps[0:BLOCKS, 4, 0:P]).then_inc(s_shift, 1)

                def take_max(k, U):
                    dve.wait_ge(s_nsc, TILES * U + k + 1)
                    dve.tensor_reduce(top[:, k // 2, k % 2:k % 2 + 1], ps[:, 4 + k % 2, :], AX.X, ALU.max
                                      ).then_inc(s_nmax, 1)
                    if k == TILES - 1:
                        dve.wait_ge(s_nmax, CREDIT + TILES * (U + 1))

                def body(u, last):
                    state["n"] = 0
                    state["base"] = chain0 + HPRE[layer] + u * per

                    def tile_value(s):
                        return CREDIT + TILES * UNIT0[layer] + u * (TILES * UNROLL) + s

                    def settle(s):
                        T, r = tile_value(s), s % RING
                        dve.wait_ge(s_exp, T + 1)
                        p = prob[:, r, :]
                        if layer == 0:
                            dve.tensor_scalar(p, p, CLIP_LO, CLIP_HI, ALU.max, ALU.min).then_inc(s_p, 1)
                        else:
                            dve.tensor_tensor(p, p, prob_b[:, r, :], ALU.max).then_inc(s_p, 1)

                    def low(s):
                        T, r = tile_value(s), s % RING
                        dve.wait_ge(s_hi, T + 1)
                        dve.wait_ge(s_exp, T + 1)
                        dve.wait_ge(s_av, T - RING + 1)
                        dve.tensor_tensor(plo[:, r, :], prob[:, r, :], phi[:, r, :], ALU.subtract
                                          ).then_inc(s_lo, 1)

                    def out_free(n, U):
                        dve.wait_ge(s_outfree, CREDIT + U - 1)

                    def blocks_done(s):
                        n, tt = s // TILES, s % TILES
                        c, j = tt // BLOCKS, tt % BLOCKS
                        acc = ps[:, 6 + s // 2 % 2, 0:2 * IB * 33].rearrange("p (a d) -> p a d", d=33)
                        dve.wait_ge(s_av, tile_value(s) + 1)
                        dve.wait_ge(s_chfree, CREDIT + u * (TILES // 2 * UNROLL) + s // 2)
                        link(dve.reciprocal(rden[:, 0:2 * IB], acc[:, :, 32]))
                        dve.tensor_tensor(blk[:, j - 1:j + 1, :, :].rearrange("p j t d -> p (j t) d"), acc[:, :, 0:32],
                                          rden[:, 0:2 * IB].unsqueeze(2).to_broadcast([P, 2 * IB, 32]),
                                          ALU.mult).then_inc(s_chfree, 1)
                        if j == BLOCKS - 1:
                            dve.wait_ge(s_chfree, CREDIT + u * (TILES // 2 * UNROLL) + s // 2 + 1)
                            U = UNIT0[layer] + u * UNROLL + n
                            if c == 0:
                                out_free(n, U)
                            ins = dve.tensor_reduce(
                                outp[:, n % 2, c * IB * 32:(c + 1) * IB * 32].rearrange("p (t d) -> p t d", d=32),
                                blk[:, :, :, :].rearrange("p j t d -> p t d j"), AX.X, ALU.add)
                            if c == 1:
                                ins.then_inc(s_out, 1)
                                dve.wait_ge(s_out, U + 1)
                            else:
                                link(ins)

                    def half_done(s):
                        n, tt = s // TILES, s % TILES
                        c = tt // BLOCKS
                        U = UNIT0[layer] + u * UNROLL + n
                        dve.wait_ge(s_av, tile_value(s) + 1)
                        if c == 0:
                            out_free(n, U)
                        banks = ((6, 2), (7, 2)) if layer == 2 else ((6 + c, IB),)
                        for m, (bank, blocks) in enumerate(banks):
                            acc = ps[:, bank, 0:blocks * (width + 1)].rearrange("p (t d) -> p t d", d=width + 1)
                            link(dve.tensor_scalar(rden[:, 0:blocks], acc[:, :, width], TINY, None, ALU.max))
                            link(dve.reciprocal(rden[:, 0:blocks], rden[:, 0:blocks]))
                            at = (c * IB + m * 2) * width
                            link(dve.tensor_tensor(
                                outp[:, n % 2, at:at + blocks * width].rearrange("p (t d) -> p t d", d=width),
                                acc[:, :, 0:width],
                                rden[:, 0:blocks].unsqueeze(2).to_broadcast([P, blocks, width]), ALU.mult))
                        dve.sem_inc(s_accfree, 1)
                        if c == 1:
                            dve.sem_inc(s_out, 1)

                    total = TILES * UNROLL
                    for s in range(total + LAG + 2):
                        if s < total:
                            if layer != 1:
                                settle(s)
                            n = s // TILES
                            if layer and not (last and n == UNROLL - 1):
                                U = SHIFT0[layer] + u * UNROLL + n + 1
                                for k in range(TILES):
                                    if SHIFT_AT[k] == s % TILES:
                                        take_max(k, U)
                                        if k == TILES - 1:
                                            find_shift((n + 1) % UNROLL)
                                if s % TILES == TURN_AT:
                                    shift_rows((n + 1) % UNROLL, U)
                        if 1 <= s <= total:
                            low(s - 1)
                        e = s - LAG - 1
                        if 0 <= e < total:
                            if layer == 0 and e % 2:
                                blocks_done(e)
                            if layer and e % BLOCKS == BLOCKS - 1:
                                half_done(e)
                    want = per - (HPRE[layer] if last else 0)
                    assert state["n"] == want, (layer, last, state["n"])

                if layer:
                    state["n"], state["base"] = 0, chain0
                    dve.wait_ge(s_stk[0], stk_at(layer, 0, 0))
                    for k in range(TILES):
                        take_max(k, SHIFT0[layer])
                    find_shift(0)
                    shift_rows(0, SHIFT0[layer])
                    assert state["n"] == HPRE[layer]
                loop(dve, layer, body)

            masks(0)
            node(0)
            heads(0)
            dve.memset(ks[96:97, :, :].bitcast(F32), 1.0).then_inc(s_krow, 1)
            masks(1)
            node(1)
            heads(1)
            masks(2)
            node(2)
            heads(2)
            masks(3)
            node(3)
            dve.wait_ge(s_cnt, 1)
            dve.tensor_scalar(empty[:, :], pf[:, 4 * HALF:6 * HALF], -BIG * NODES, None, ALU.is_equal
                              ).then_inc(s_empty, 1)
            heads(3)
            node(4)


_WEIGHTS = ("L0_gnn_Wq", "L0_gnn_Wk", "L0_gnn_Wv", "L0_gnn_Wo", "L1_gnn_wq", "L1_gnn_wk", "L1_gnn_wv", "L1_gnn_wo")
_ROWS = ("L0_gnn_bv", "L0_gnn_bo", "L1_gnn_bv", "L1_gnn_bo", "L0_gnn_gamma", "L0_gnn_beta")
_COLS = ("L0_gnn_bq", "L0_gnn_bk", "L1_gnn_bq", "L1_gnn_bk")


def kernel(**inputs):
    import numpy as np
    import concourse.bacc as bacc
    from concourse import mybir as _mybir
    from concourse.bass_utils import run_bass_kernel_spmd

    a = {n: np.asarray(v) for n, v in inputs.items()}
    arrays = {"x": a["x"], "adj_n": a["adj"], "adj_t": a["adj"].T}
    for n in _WEIGHTS:
        arrays[n] = a[n].T
    for n in _ROWS:
        arrays[n] = np.broadcast_to(a[n], (P, F))
    for n in _COLS:
        arrays[n] = a[n].reshape(F, 1)
    arrays["L2_gnn_W"] = a["L2_gnn_W"]
    arrays["L2_gnn_a"] = a["L2_gnn_a"].reshape(2, F).T
    arrays["L3_gnn_W"] = a["L3_gnn_W"].transpose(1, 0, 2).reshape(F, F)
    side = np.zeros((4, 32, 2, 4), a["L3_gnn_a"].dtype)
    for h in range(4):
        side[h, :, 0, h] = a["L3_gnn_a"][h, :32]
        side[h, :, 1, h] = a["L3_gnn_a"][h, 32:]
    arrays["L3_gnn_a"] = side.reshape(F, 8)
    arrays = {n: np.ascontiguousarray(v) for n, v in arrays.items()}

    nc = bacc.Bacc("TRN2", target_bir_lowering=False, num_devices=1)
    t = {n: nc.dram_tensor("in_" + n, v.shape, _mybir.dt.from_np(v.dtype), kind="ExternalInput").ap()
         for n, v in arrays.items()}
    t["out"] = nc.dram_tensor("out_0", (GRAPHS, NODES, F), F32, kind="ExternalOutput").ap()
    build(nc, t)
    r = run_bass_kernel_spmd(nc, [{"in_" + n: v for n, v in arrays.items()}], core_ids=[0])
    return r.results[0]["out_0"]
```

```python
from contextlib import ExitStack

import concourse.bass as bass
from concourse import mybir

F32 = mybir.dt.float32
F32R = mybir.dt.float32r
BF16 = mybir.dt.bfloat16
F16 = mybir.dt.float16
I32 = mybir.dt.int32
ALU = mybir.AluOpType
ACT = mybir.ActivationFunctionType
AX = mybir.AxisListType

P = 128
GRAPHS, NODES, F = 8, 1024, 128
BLOCKS = NODES // P
HALF = 512
IB = HALF // P
TILES = BLOCKS * 2
LAYERS = 4
HEADS = (4, 4, 1, 4)
WIDTH = tuple(F // h for h in HEADS)
UNITS = tuple(GRAPHS * h for h in HEADS)
UNIT0 = tuple(sum(UNITS[:n]) for n in range(LAYERS))
SHIFT0 = tuple(sum(UNITS[1:n]) for n in range(LAYERS))
BIG = 2.0 ** 100
LEAST = -(2.0 ** 66)
TINY = 2.0 ** -100
EPS = 1e-5
SLOPE = 0.2
SCALE = 32.0 ** -0.5
LN2 = 0.6931471805599453
CLIP_LO = 2.0 * 4.5399929762484854e-05
CLIP_HI = 2.0 * 22026.465794806718
UNROLL = 4
RING = 4
CREDIT = 32
SHIFT_CREDIT = 1
LAG = 3
SHIFT_AT = [k * 3 // 4 for k in range(TILES)]
TURN_AT = 14
V3 = 3 * 33
V3W = 3 * 129
LOADS = (9, 7, 9, 10)
ROWMS = (0, 1, 2, 2)
CHAIN_A = (0, 9, 3, 4, 4)
CHAIN_B = (3, 3, 7, 12)
HCHAIN = (36, 28, 68, 44)
HPRE = (0, 1, 5, 5)
NODE_LOADS = (1, 5, 5, 2, 5)
PART_STORES = (5, 5, 6, 7)


def build(nc, t):
    with ExitStack() as ctx:
        def sb(name, shape, dt=F32):
            return ctx.enter_context(nc.sbuf_tensor(name, shape, dt))

        def sem(name):
            return ctx.enter_context(nc.semaphore(name))

        ps = ctx.enter_context(nc.psum_tensor("ps", [P, 8, HALF], F32))
        pf = ps[:, :, :].rearrange("p b n -> p (b n)")

        x_d = nc.dram_tensor("x_d", (GRAPHS, P, BLOCKS, F), F32, kind="Internal").ap()
        ctx_d = nc.dram_tensor("ctx_d", (GRAPHS * 4, P, BLOCKS, 32), F32, kind="Internal").ap()
        ctx2_d = nc.dram_tensor("ctx2_d", (GRAPHS, P, BLOCKS * F), F32, kind="Internal").ap()
        q_d = nc.dram_tensor("q_d", (2, GRAPHS * 4 * 32, NODES), F32, kind="Internal").ap()
        k_d = nc.dram_tensor("k_d", (2, GRAPHS * 4 * 32, NODES), F32, kind="Internal").ap()
        v_d = nc.dram_tensor("v_d", (GRAPHS * 4, P, BLOCKS * V3), BF16, kind="Internal").ap()
        v2_d = nc.dram_tensor("v2_d", (GRAPHS, P, BLOCKS * V3W), BF16, kind="Internal").ap()
        row_d = nc.dram_tensor("row_d", (4, GRAPHS * 8, NODES), F32, kind="Internal").ap()
        col_d = nc.dram_tensor("col_d", (GRAPHS * 8, P, BLOCKS), F32, kind="Internal").ap()
        sum_d = nc.dram_tensor("sum_d", (GRAPHS * 4, P, V3), BF16, kind="Internal").ap()

        ident = sb("ident", [P, P])
        ident_b = sb("ident_b", [P, P], BF16)
        ones_b = sb("ones_b", [P, P], BF16)
        expo = sb("expo", [P, BLOCKS])
        ln2 = sb("ln2", [P, 1])
        anti = sb("anti", [P, P], BF16)
        wts = sb("wts", [P, 10, F])
        rows = sb("rows", [P, 6, F])
        bcol = sb("bcol", [P, 4])
        aa = sb("aa", [P, 2, 8])
        mask_n = sb("mask_n", [P, BLOCKS, NODES], BF16)
        mask_t = sb("mask_t", [P, BLOCKS, NODES], BF16)
        empty = sb("empty", [P, NODES], BF16)

        diag = sb("diag", [P, 2, BLOCKS, P], BF16)
        adj_i = sb("adj_i", [P, 4, NODES], I32)
        sel = sb("sel", [P, 2, P], F32R)

        xr = sb("xr", [P, 2, BLOCKS, F])
        cs = sb("cs", [P, 2, BLOCKS, F])
        work = sb("work", [P, BLOCKS, F])
        neg = sb("neg", [P, BLOCKS, F])
        xn = sb("xn", [P, 2, BLOCKS, F])
        cT = sb("cT", [P, NODES])
        xT = sb("xT", [P, NODES])
        bns = sb("bns", [P, BLOCKS, 6])
        mv = sb("mv", [P, BLOCKS, 2])
        var = sb("var", [P, BLOCKS])
        rstd = sb("rstd", [P, BLOCKS])
        full = sb("full", [P, 2, NODES])
        part = sb("part", [P, 2, 2, NODES], F32R)
        rowp = part[0:8, :, :, :].rearrange("p a b n -> p (a b) n")
        vf = sb("vf", [P, BLOCKS, F])
        vbuf = sb("vbuf", [P, 4, BLOCKS, 3, 33], BF16)
        v2buf = sb("v2buf", [P, BLOCKS, 3, 129], BF16)
        vsum = sb("vsum", [P, F])
        vsumb = sb("vsumb", [P, 4, 3, 33], BF16)
        colp = sb("colp", [P, 8, BLOCKS])

        qs = sb("qs", [P, UNROLL, NODES], F32R)
        ks = sb("ks", [P, UNROLL, NODES], F32R)
        vs = sb("vs", [P, UNROLL, BLOCKS * V3W], BF16)
        zs = sb("zs", [P, UNROLL, V3], BF16)
        cols = sb("cols", [P, UNROLL, 2, BLOCKS])
        cols2 = sb("cols2", [P, UNROLL, BLOCKS])
        prob = xr[:, :, :, :].rearrange("p a t f -> p (a t f)").rearrange("p (r n) -> p r n", n=HALF)
        prob_b = cs[:, :, :, :].rearrange("p a t f -> p (a t f)").rearrange("p (r n) -> p r n", n=HALF)
        phi = cT[:, :].bitcast(F16).rearrange("p (r n) -> p r n", n=HALF)
        plo = xT[:, :].bitcast(BF16).rearrange("p (r n) -> p r n", n=HALF)
        top = sb("top", [P, BLOCKS, 2])
        shift = sb("shift", [P, 3, BLOCKS])
        nshift = sb("nshift", [P, 2, BLOCKS])
        shrow = sb("shrow", [BLOCKS, 2, P], F32R)
        rden = sb("rden", [P, 8])
        blk = work[:, :, :].rearrange("p j (t d) -> p j t d", d=32)
        outp = xn[:, :, :, :].rearrange("p a t f -> p a (t f)")

        s_const = sem("s_const")
        s_ident = sem("s_ident")
        s_fill = sem("s_fill")
        s_krow = sem("s_krow")
        s_anti = sem("s_anti")
        s_adj = [sem(f"s_adj{n}") for n in range(4)]
        s_mask = sem("s_mask")
        s_diag = sem("s_diag")
        s_zero = sem("s_zero")
        s_sel = sem("s_sel")
        s_cnt = sem("s_cnt")
        s_empty = sem("s_empty")
        s_load = [sem("s_load0"), sem("s_load1")]
        s_xst = [sem("s_xst0"), sem("s_xst1")]
        s_pst = sem("s_pst")
        s_chain_a = sem("s_chain_a")
        s_chain_b = sem("s_chain_b")
        s_stats = sem("s_stats")
        s_hchain = sem("s_hchain")
        s_stk = [sem(f"s_stk{n}") for n in range(UNROLL)]
        s_rowm = [sem(f"s_rowm{n}") for n in range(UNROLL)]
        s_cols2 = sem("s_cols2")
        s_score = sem("s_score")
        s_exp = sem("s_exp")
        s_p = sem("s_p")
        s_hi = sem("s_hi")
        s_lo = sem("s_lo")
        s_av = sem("s_av")
        s_accfree = sem("s_accfree")
        s_chfree = sem("s_chfree")
        s_nsc = sem("s_nsc")
        s_nmax = sem("s_nmax")
        s_shcol = sem("s_shcol")
        s_shT = sem("s_shT")
        s_shift = sem("s_shift")
        s_out = sem("s_out")
        s_ctx = sem("s_ctx")
        s_outfree = sem("s_outfree")
        EVENTS = {
            "cT_ps": (1, 2),
            "cT": (1, 2),
            "y_ps": (1, 2),
            "y": (1, 2),
            "eneg": (3, 4),
            "eexp": (3, 4),
            "var": (1, 2, 3, 4),
            "rstd": (1, 2, 3, 4),
            "var0": (1,),
            "rstd0": (1,),
            "xn": (1, 2, 3, 4),
            "xT_ps": (0, 1, 2, 3),
            "xT": (0, 1, 2, 3),
            "q_ps": (0, 1),
            "k_ps": (0, 1),
            "w_ps": (2, 3),
            "v_ps": (0, 1, 2, 3),
            "row_ps": (2, 3),
            "q": (0, 1),
            "k": (0, 1),
            "w": (2, 3),
            "row": (2, 3),
            "col": (2, 3),
            "q2": (0, 1),
            "k2": (0, 1),
            "row2": (2, 3),
            "vf": (0, 1, 2, 3),
            "v": (0, 1, 2, 3),
        }
        s_ev = {name: sem("s_" + name) for name in EVENTS}

        def ev(name, stage, b):
            assert stage in EVENTS[name]
            return 2 + GRAPHS * EVENTS[name].index(stage) + b

        def before(name, stage, b):
            if stage in EVENTS[name]:
                return 1 + GRAPHS * EVENTS[name].index(stage) + b
            return 1 + GRAPHS * sum(s < stage for s in EVENTS[name])

        def load_at(stage, h):
            return 16 * (GRAPHS // 2) * sum(NODE_LOADS[:stage]) + (h + 1) * (16 * NODE_LOADS[stage])

        def xst_before(stage, h):
            return 16 + 16 * (GRAPHS // 2) * max(stage - 1, 0) + h * 16

        def pst_before(stage, b):
            return 16 + 16 * GRAPHS * sum(PART_STORES[:stage]) + b * (16 * PART_STORES[stage])

        def stk_at(layer, n, u):
            return 16 * sum(LOADS[m] * UNITS[m] // UNROLL for m in range(layer)) + (u + 1) * (16 * LOADS[layer])

        def rowm_at(layer, n, u):
            return 16 * sum(ROWMS[m] * UNITS[m] // UNROLL for m in range(layer)) + (u + 1) * (16 * ROWMS[layer])

        def loop(eng, layer, body):
            n = UNITS[layer] // UNROLL
            if n - 1 > 1:
                with eng.Fori(0, n - 1) as u:
                    body(u, False)
            else:
                body(0, False)
            body(n - 1, True)

        def graphs(eng, finish, project):
            finish(0, 0, 0)
            with eng.Fori(0, GRAPHS // 2 - 1) as h:
                finish(h * 2 + 1, 1, h)
                project(h * 2, 0, h)
                finish(h * 2 + 2, 0, h + 1)
                project(h * 2 + 1, 1, h)
            h = GRAPHS // 2 - 1
            finish(2 * h + 1, 1, h)
            project(2 * h, 0, h)
            project(2 * h + 1, 1, h)

        x_in = t["x"].rearrange("b (t p) f -> b p t f", p=P)
        x_out = t["out"].rearrange("b (t p) f -> b p t f", p=P)

        def one(ap, i):
            return ap[bass.ds(i, 1)]

        block = ctx.enter_context(nc.Block())

        @block.sync
        def _(sp):
            for k, name in enumerate(("L0_gnn_Wq", "L0_gnn_Wk", "L0_gnn_Wv", "L0_gnn_Wo",
                                      "L1_gnn_wq", "L1_gnn_wk", "L1_gnn_wv", "L1_gnn_wo",
                                      "L2_gnn_W", "L3_gnn_W")):
                sp.dma_start(wts[:, k, :], t[name]).then_inc(s_const, 16)
            for k, name in enumerate(("L0_gnn_bv", "L0_gnn_bo", "L1_gnn_bv", "L1_gnn_bo",
                                      "L0_gnn_gamma", "L0_gnn_beta")):
                sp.dma_start(rows[:, k, :], t[name]).then_inc(s_const, 16)
            for k, name in enumerate(("L0_gnn_bq", "L0_gnn_bk", "L1_gnn_bq", "L1_gnn_bk")):
                sp.dma_start(bcol[:, k:k + 1], t[name]).then_inc(s_const, 16)
            sp.dma_start(aa[:, 0, 0:2], t["L2_gnn_a"]).then_inc(s_const, 16)
            sp.dma_start(aa[:, 1, :], t["L3_gnn_a"]).then_inc(s_const, 16)

            def load_graph(stage, b, q, h):
                src = one(x_in if stage < 2 else x_d, b).rearrange("a p t f -> (a p) t f")
                if stage == 0:
                    if not (isinstance(b, int) and b < 2):
                        sp.wait_ge(s_ev["xT_ps"], ev("xT_ps", stage, b) - 2)
                    sp.dma_start(xn[:, q, :, :], src).then_inc(s_load[q], 16)
                    return
                sp.dma_start(xr[:, q, :, :], src).then_inc(s_load[q], 16)
                if stage == 3:
                    sp.dma_start(cs[:, q, :, :].rearrange("p t f -> p (t f)"),
                                 one(ctx2_d, b).rearrange("a p n -> (a p) n")).then_inc(s_load[q], 16)
                else:
                    for k in range(4):
                        sp.dma_start(cs[:, q, :, 32 * k:32 * k + 32],
                                     one(ctx_d, b * 4 + k).rearrange("a p t f -> (a p) t f")
                                     ).then_inc(s_load[q], 16)

            def node(stage):
                def finish(b, q, h):
                    if isinstance(b, int) and b == 0:
                        load_graph(stage, 0, 0, 0)
                        load_graph(stage, 1, 1, 0)
                    if stage:
                        sp.wait_ge(s_ev["xn"], ev("xn", stage, b))
                        dst = x_out if stage == 4 else x_d
                        sp.dma_start(one(dst, b).rearrange("a p t f -> (a p) t f"), xn[:, q, :, :]
                                     ).then_inc(s_xst[q], 16)
                    load_graph(stage, b + 2, q, h + 1)

                def project(b, q, h):
                    if stage == 4:
                        return
                    if stage < 2:
                        for w, (name, dst) in enumerate((("q2", q_d), ("k2", k_d))):
                            sp.wait_ge(s_ev[name], ev(name, stage, b))
                            for s in range(2):
                                sp.dma_start(dst[s, bass.ds(b * P, P)], part[:, w, s, :].bitcast(F32)
                                             ).then_inc(s_pst, 16)
                    else:
                        n = 2 * HEADS[stage]
                        sp.wait_ge(s_ev["row2"], ev("row2", stage, b))
                        for kind in range(4):
                            sp.dma_start(row_d[kind, bass.ds(b * 8, n)], rowp[0:n, kind, :].bitcast(F32)
                                         ).then_inc(s_pst, 16)
                        sp.dma_start(col_d[bass.ds(b * 8, n)].rearrange("r p t -> p r t"), colp[:, 0:n, :]
                                     ).then_inc(s_pst, 16)
                    sp.wait_ge(s_ev["v"], ev("v", stage, b))
                    if stage == 2:
                        sp.dma_start(one(v2_d, b).rearrange("a p n -> (a p) n"),
                                     v2buf[:, :, :, :].rearrange("p t s d -> p (t s d)")).then_inc(s_pst, 16)
                    else:
                        sp.dma_start(v_d[bass.ds(b * 4, 4)].rearrange("h p n -> p h n"),
                                     vbuf[:, :, :, :, :].rearrange("p h t s d -> p h (t s d)")
                                     ).then_inc(s_pst, 16)
                    if stage == 3:
                        sp.dma_start(sum_d[bass.ds(b * 4, 4)].rearrange("h p n -> p h n"),
                                     vsumb[:, :, :, :].rearrange("p h s d -> p h (s d)")).then_inc(s_pst, 16)

                finish(0, 0, 0)
                with sp.Fori(0, GRAPHS // 2 - 2) as h:
                    finish(h * 2 + 1, 1, h)
                    project(h * 2, 0, h)
                    finish(h * 2 + 2, 0, h + 1)
                    project(h * 2 + 1, 1, h)
                h = GRAPHS // 2 - 2
                finish(2 * h + 1, 1, h)
                project(2 * h, 0, h)
                store_last(stage, 2 * h + 2, 0)
                project(2 * h + 1, 1, h)
                store_last(stage, 2 * h + 3, 1)
                project(2 * h + 2, 0, h + 1)
                project(2 * h + 3, 1, h + 1)
                if stage:
                    for q in range(2):
                        sp.wait_ge(s_xst[q], xst_before(stage, GRAPHS // 2))
                if stage < 4:
                    sp.wait_ge(s_pst, pst_before(stage, GRAPHS))

            def store_last(stage, b, q):
                if stage:
                    sp.wait_ge(s_ev["xn"], ev("xn", stage, b))
                    dst = x_out if stage == 4 else x_d
                    sp.dma_start(one(dst, b).rearrange("a p t f -> (a p) t f"), xn[:, q, :, :]
                                 ).then_inc(s_xst[q], 16)

            def load_unit(layer, u, m):
                g, n = u * UNROLL + m, m % UNROLL
                count = 0

                def go(dst, src):
                    nonlocal count
                    count += 1
                    sp.dma_start(dst, src).then_inc(s_stk[n], 16)

                if layer < 2:
                    for r, (a, c) in enumerate(((0, 0), (0, 1), (1, 0), (1, 1))[:4 - layer]):
                        go(qs[32 * r:32 * r + 32, n, :].bitcast(F32), q_d[a, bass.ds(g * 32, 32)])
                        go(ks[32 * r:32 * r + 32, n, :].bitcast(F32), k_d[c, bass.ds(g * 32, 32)])
                    go(vs[:, n, 0:BLOCKS * V3], one(v_d, g).rearrange("a p n -> (a p) n"))
                else:
                    heads = HEADS[layer]
                    r = g * 8 if heads == 1 else (u + m // UNROLL) * 8 + n
                    for k in range(2):
                        go(qs[k:k + 1, n, :].bitcast(F32), row_d[k, bass.ds(r, 1)])
                        go(ks[k:k + 1, n, :].bitcast(F32), row_d[2 + k, bass.ds(r, 1)])
                        go(ks[32 + k:33 + k, n, :].bitcast(F32), row_d[k, bass.ds(r + heads, 1)])
                    for k in range(2):
                        go(cols[:, n, k, :], one(col_d, r + k * heads).rearrange("a p t -> (a p) t"))
                    if layer == 2:
                        go(vs[:, n, :], one(v2_d, g).rearrange("a p n -> (a p) n"))
                    else:
                        go(vs[:, n, 0:BLOCKS * V3], one(v_d, g).rearrange("a p n -> (a p) n"))
                        go(zs[:, n, :], one(sum_d, g).rearrange("a p n -> (a p) n"))
                assert count == LOADS[layer]

            def place_shift(layer, g, n):
                sp.wait_ge(s_shift, SHIFT_CREDIT + SHIFT0[layer] + g + 1)
                for dst in ((qs[96:97, n, :],) if layer == 1 else (qs[2:3, n, :], ks[2:3, n, :])):
                    sp.dma_start(dst.bitcast(F32).rearrange("a (t p) -> a t p", p=P),
                                 shrow[:, n % 2, :].bitcast(F32)).then_inc(s_rowm[n], 16)

            def heads(layer):
                if layer == 2:
                    sp.wait_ge(s_zero, 2)
                for n in range(2):
                    load_unit(layer, 0, n)
                if layer:
                    place_shift(layer, 0, 0)

                def body(u, last):
                    for n in range(UNROLL):
                        g = u * UNROLL + n
                        if not (last and n >= UNROLL - 2):
                            sp.wait_ge(s_av, CREDIT + TILES * (UNIT0[layer] - 1) + g * TILES)
                            load_unit(layer, u, n + 2)
                        if layer and not (last and n == UNROLL - 1):
                            place_shift(layer, g + 1, (n + 1) % UNROLL)

                loop(sp, layer, body)
                sp.wait_ge(s_outfree, CREDIT + UNIT0[layer] + UNITS[layer])

            node(0)
            heads(0)
            node(1)
            heads(1)
            node(2)
            heads(2)
            node(3)
            heads(3)
            node(4)

        @block.gpsimd
        def _(pool):
            pool.memset(ident[:, :], 0.0).then_inc(s_ident, 1)
            pool.memset(ident_b[:, :], 0.0).then_inc(s_ident, 1)
            pool.memset(expo[:, :], -0.5).then_inc(s_ident, 1)
            pool.wait_ge(s_ident, 3)
            for m in (ident, ident_b):
                pool.affine_select(out=m[:, :], in_=m[:, :], compare_op=ALU.not_equal, fill=1.0, base=0,
                                   pattern=[[-1, P]], channel_multiplier=1).then_inc(s_ident, 1)
            pool.memset(anti[:, :], 1.0).then_inc(s_anti, 1)
            pool.wait_ge(s_anti, 1)
            pool.affine_select(out=anti[:, :], in_=anti[:, :], compare_op=ALU.not_equal, fill=0.0, base=0,
                               pattern=[[-1, P]], channel_multiplier=1).then_inc(s_anti, 1)
            pool.sem_inc(s_outfree, CREDIT)
            for s in (*s_xst, s_pst):
                pool.sem_inc(s, 16)
            for name in ("rstd", "rstd0"):
                pool.sem_inc(s_ev[name], 1)

            def load_adj(first, k):
                src = t["adj_n" if k % 2 else "adj_t"]
                pool.dma_start(adj_i[:, k % 4, :], src[k // 2 * P:(k // 2 + 1) * P, :]).then_inc(s_adj[k % 4], 16)

            def mask_block(first, k):
                pool.wait_ge(s_adj[k % 4], 16 * (4 * first + k // 4 + 1))
                dst = (mask_n if k % 2 else mask_t)[:, k // 2, :]
                pool.tensor_scalar(dst, adj_i[:, k % 4, :], 0.0, -BIG, ALU.is_le if first else ALU.is_equal,
                                   ALU.mult).then_inc(s_mask, 1)
                pool.wait_ge(s_mask, 16 * first + k + 1)
                if k + 4 < 2 * BLOCKS:
                    load_adj(first, k + 4)

            def diagonal(k):
                d = (mask_n if k % 2 else mask_t)[:, k // 2, k // 2 * P:(k // 2 + 1) * P]
                keep = diag[:, k % 2, k // 2, :]
                pool.tensor_copy(keep, d).then_inc(s_diag, 1)
                pool.wait_ge(s_diag, 2 * k + 1)
                pool.tensor_tensor(d, keep, anti[:, :], ALU.mult).then_inc(s_diag, 1)
                pool.wait_ge(s_diag, 2 * k + 2)

            def power(stage, name, b):
                pool.wait_ge(s_ev["var" + name], ev("var" + name, stage, b))
                pool.tensor_tensor(rstd[:, :], var[:, :], expo[:, :], ALU.pow).then_inc(s_ev["rstd" + name], 1)

            def node(stage):
                if stage == 2:
                    for k in range(4):
                        load_adj(1, k)
                if stage != 2:
                    with pool.Fori(0, GRAPHS) as b:
                        if stage == 1:
                            power(stage, "0", b)
                        power(stage, "", b)
                    return
                for b in range(GRAPHS):
                    power(stage, "", b)
                    for k in range(2 * b, 2 * b + 2):
                        mask_block(1, k)
                        diagonal(k)

            def heads(layer):
                def body(u, last):
                    for n in range(UNROLL):
                        g = u * UNROLL + n
                        pool.wait_ge(s_out, UNIT0[layer] + g + 1)
                        if layer == 2:
                            pool.dma_start(one(ctx2_d, g).rearrange("a p n -> (a p) n"), outp[:, n % 2, :]
                                           ).then_inc(s_ctx, 16)
                        else:
                            pool.dma_start(one(ctx_d, g).rearrange("a p t f -> (a p) (t f)"),
                                           outp[:, n % 2, 0:BLOCKS * 32]).then_inc(s_ctx, 16)
                        pool.wait_ge(s_ctx, 16 * (UNIT0[layer] + 1) + g * 16)
                        pool.sem_inc(s_outfree, 1)

                loop(pool, layer, body)

            for k in range(4):
                load_adj(0, k)
            for k in range(2 * BLOCKS):
                mask_block(0, k)
            heads(0)
            pool.memset(ks[96:97, :, :].bitcast(F32), 1.0).then_inc(s_krow, 1)
            pool.wait_ge(s_krow, 1)
            node(1)
            heads(1)
            pool.memset(qs[:, :, :].bitcast(F32), 0.0).then_inc(s_zero, 1)
            pool.memset(ks[:, :, :].bitcast(F32), 0.0).then_inc(s_zero, 1)
            node(2)
            heads(2)
            for k in range(2 * BLOCKS):
                d = (mask_n if k % 2 else mask_t)[:, k // 2, k // 2 * P:(k // 2 + 1) * P]
                pool.tensor_copy(d, diag[:, k % 2, k // 2, :]).then_inc(s_diag, 1)
            node(3)
            heads(3)
            node(4)

        @block.scalar
        def _(act):
            for name in ("cT", "eexp", "xT", "q", "k", "w", "row"):
                act.sem_inc(s_ev[name], 1)
            act.sem_inc(s_exp, CREDIT)
            act.sem_inc(s_hi, CREDIT)
            act.wait_ge(s_const, 16 * 22)

            def node(stage):
                def finish(b, q, h):
                    if stage in (1, 2):
                        act.wait_ge(s_ev["cT_ps"], ev("cT_ps", stage, b))
                        act.wait_ge(s_ev["y_ps"], before("y_ps", stage, b))
                        act.activation(cT[:, :], pf[:, 0:NODES], ACT.Copy).then_inc(s_ev["cT"], 1)
                    if stage in (3, 4):
                        act.wait_ge(s_ev["eneg"], ev("eneg", stage, b))
                        act.activation(neg[:, :, :], neg[:, :, :], ACT.Exp).then_inc(s_ev["eexp"], 1)

                def project(b, q, h):
                    if stage == 4:
                        return
                    act.wait_ge(s_ev["xT_ps"], ev("xT_ps", stage, b))
                    act.wait_ge(s_ev["v_ps"], before("v_ps", stage, b))
                    act.activation(xT[:, :], pf[:, 4 * HALF:6 * HALF], ACT.Copy).then_inc(s_ev["xT"], 1)
                    if stage < 2:
                        act.wait_ge(s_pst, pst_before(stage, b))
                        for w, name in enumerate("qk"):
                            act.wait_ge(s_ev[name + "_ps"], ev(name + "_ps", stage, b))
                            act.activation(part[:, w, 0, :], pf[:, (6 - 2 * w) * HALF:(8 - 2 * w) * HALF],
                                           ACT.Identity, bias=bcol[:, 2 * stage + w:2 * stage + w + 1]
                                           ).then_inc(s_ev[name], 1)
                        return
                    n = 2 * HEADS[stage]
                    act.wait_ge(s_ev["w_ps"], ev("w_ps", stage, b))
                    act.wait_ge(s_ev["row_ps"], before("row_ps", stage, b))
                    act.activation(full[:, 0, :], pf[:, 6 * HALF:8 * HALF], ACT.Copy).then_inc(s_ev["w"], 1)
                    act.wait_ge(s_ev["row_ps"], ev("row_ps", stage, b))
                    act.wait_ge(s_ev["row2"], before("row2", stage, b))
                    act.activation(full[0:n, 1, :], pf[0:n, 4 * HALF:6 * HALF], ACT.Copy).then_inc(s_ev["row"], 1)

                graphs(act, finish, project)

            def heads(layer):
                def body(u, last):
                    def tile_value(s):
                        return CREDIT + TILES * UNIT0[layer] + u * (TILES * UNROLL) + s

                    def exps(s):
                        n, j, r = s // TILES, s % BLOCKS, s % RING
                        T = tile_value(s)
                        act.wait_ge(s_score, T - CREDIT + 1)
                        act.wait_ge(s_lo, T - RING + 1)
                        if layer == 0:
                            act.activation(prob[:, r, :], ps[:, r, :], ACT.Exp, scale=SCALE, bias=ln2[:, 0:1]
                                           ).then_inc(s_exp, 1)
                        elif layer == 1:
                            act.activation(prob[:, r, :], ps[:, r, :], ACT.Exp, scale=SCALE).then_inc(s_exp, 1)
                            act.wait_ge(s_av, T - RING + 1)
                            act.activation(phi[:, r, :], ps[:, r, :], ACT.Exp, scale=SCALE).then_inc(s_hi, 1)
                        else:
                            y = 2 * (s % 2)
                            if j == 0:
                                act.wait_ge(s_cols2, UNIT0[layer] - UNIT0[2] + u * UNROLL + n + 1)
                            act.activation(prob[:, r, :], ps[:, y, :], ACT.Exp, bias=cols[:, n, 1, j:j + 1])
                            act.activation(prob_b[:, r, :], ps[:, y + 1, :], ACT.Exp, bias=cols2[:, n, j:j + 1]
                                           ).then_inc(s_exp, 1)

                    def high(s):
                        T, r = tile_value(s), s % RING
                        act.wait_ge(s_p, T - CREDIT + 1 - (TILES * UNITS[1] if layer > 1 else 0))
                        act.wait_ge(s_av, T - RING + 1)
                        act.activation(phi[:, r, :], prob[:, r, :], ACT.Copy).then_inc(s_hi, 1)

                    for s in range(TILES * UNROLL + 1):
                        if s < TILES * UNROLL:
                            exps(s)
                        if s and layer != 1:
                            high(s - 1)

                loop(act, layer, body)

            act.wait_ge(s_fill, 8)
            node(0)
            heads(0)
            node(1)
            heads(1)
            node(2)
            heads(2)
            node(3)
            heads(3)
            node(4)

        @block.tensor
        def _(pe):
            for name in ("cT_ps", "y_ps", "xT_ps", "q_ps", "k_ps", "w_ps", "v_ps", "row_ps"):
                pe.sem_inc(s_ev[name], 1)
            pe.sem_inc(s_av, CREDIT)
            pe.wait_ge(s_const, 16 * 22)
            pe.wait_ge(s_ident, 5)
            pe.wait_ge(s_fill, 8)
            pe.wait_ge(s_sel, 3)

            def node(stage):
                def finish(b, q, h):
                    if stage not in (1, 2):
                        return
                    wo = wts[:, 4 * (stage - 1) + 3, :]
                    pe.wait_ge(s_load[q], load_at(stage, h))
                    if stage == 2:
                        pe.wait_ge(s_ev["col"], before("col", stage, b) - 1)
                    for it in range(BLOCKS):
                        mm = pe.transpose(pf[:, it * P:(it + 1) * P], cs[:, q, it, :], ident[:, :])
                    mm.then_inc(s_ev["cT_ps"], 1)
                    pe.wait_ge(s_ev["cT"], ev("cT", stage, b))
                    pe.wait_ge(s_ev["y"], before("y", stage, b))
                    for it in range(BLOCKS):
                        mm = pe.matmul(pf[:, 2 * HALF + it * P:2 * HALF + (it + 1) * P],
                                       cT[:, it * P:(it + 1) * P], wo, start=True, stop=True)
                    mm.then_inc(s_ev["y_ps"], 1)

                def project(b, q, h):
                    if stage < 2:
                        pe.wait_ge(s_ev["k2"], before("k2", stage, b))
                    else:
                        pe.wait_ge(s_ev["row"], before("row", stage, b))
                    if stage == 0:
                        pe.wait_ge(s_load[q], load_at(stage, h))
                    else:
                        pe.wait_ge(s_ev["xn"], ev("xn", stage, b))
                    for it in range(BLOCKS):
                        mm = pe.transpose(pf[:, 4 * HALF + it * P:4 * HALF + (it + 1) * P], xn[:, q, it, :],
                                          ident[:, :])
                    mm.then_inc(s_ev["xT_ps"], 1)
                    pe.wait_ge(s_ev["xT"], ev("xT", stage, b))
                    pe.wait_ge(s_ev["vf"], before("vf", stage, b))
                    if stage < 2:
                        for w, name in enumerate("qk"):
                            for c in range(2):
                                mm = pe.matmul(ps[:, 6 - 2 * w + c, :], wts[:, 4 * stage + w, :],
                                               xT[:, c * HALF:(c + 1) * HALF], start=True, stop=True)
                            mm.then_inc(s_ev[name + "_ps"], 1)
                        wv = wts[:, 4 * stage + 2, :]
                        pe.wait_ge(s_ev["q2"], ev("q2", stage, b))
                    else:
                        n, wv = 2 * HEADS[stage], wts[:, 6 + stage, :]
                        a = aa[:, stage - 2, 0:n]
                        for c in range(2):
                            mm = pe.matmul(ps[:, 6 + c, :], wv, xT[:, c * HALF:(c + 1) * HALF],
                                           start=True, stop=True)
                        mm.then_inc(s_ev["w_ps"], 1)
                        pe.wait_ge(s_ev["w"], ev("w", stage, b))
                        pe.wait_ge(s_ev["col"], before("col", stage, b))
                        for c in range(2):
                            pe.matmul(ps[0:n, 4 + c, :], a, full[:, 0, c * HALF:(c + 1) * HALF],
                                      start=True, stop=True)
                        for it in range(BLOCKS):
                            mm = pe.matmul(ps[:, 0, it * n:(it + 1) * n], full[:, 0, it * P:(it + 1) * P], a,
                                           start=True, stop=True)
                        mm.then_inc(s_ev["row_ps"], 1)
                    for it in range(BLOCKS):
                        mm = pe.matmul(pf[:, 6 * HALF + it * P:6 * HALF + (it + 1) * P],
                                       xT[:, it * P:(it + 1) * P], wv, start=True, stop=True)
                    mm.then_inc(s_ev["v_ps"], 1)

                graphs(pe, finish, project)

            def heads(layer):
                width = WIDTH[layer] + 1

                def unit_ready(n, u):
                    pe.wait_ge(s_stk[n], stk_at(layer, n, u))

                def top_scores(n, k, U):
                    it, c = k // 2, k % 2
                    bank = ps[:, 4 + k % 2, :]
                    pe.wait_ge(s_nmax, CREDIT + TILES * U + k - 1)
                    if k == 0:
                        pe.wait_ge(s_shift, SHIFT_CREDIT + U)
                    cut = slice(c * HALF, (c + 1) * HALF)
                    pe.matmul(bank, ident_b[:, :], mask_n[:, it, cut], start=True, stop=False)
                    if layer == 1:
                        mm = pe.matmul(bank, qs[0:96, n, it * P:(it + 1) * P], ks[0:96, n, cut],
                                       start=False, stop=True)
                    else:
                        mm = pe.matmul(bank, sel[:, 1, :], ks[:, n, cut], start=False, stop=True)
                    mm.then_inc(s_nsc, 1)

                def turn_shift(n, U):
                    pe.wait_ge(s_shcol, U + 1)
                    pe.transpose(ps[0:BLOCKS, 4, 0:P], nshift[:, n % 2, :], ident[:, :]).then_inc(s_shT, 1)

                def body(u, last):
                    def tile_value(s):
                        return CREDIT + TILES * UNIT0[layer] + u * (TILES * UNROLL) + s

                    def scores(s):
                        n, tt = s // TILES, s % TILES
                        c, j = tt // BLOCKS, tt % BLOCKS
                        cut, blk_j = slice(c * HALF, (c + 1) * HALF), slice(j * P, (j + 1) * P)
                        T = tile_value(s)
                        if tt == 0:
                            unit_ready(n, u)
                            if layer:
                                pe.wait_ge(s_rowm[n], rowm_at(layer, n, u))
                        if layer < 2:
                            bank = ps[:, s % RING, :]
                            pe.wait_ge(s_exp if layer == 0 else s_hi, T - RING + 1)
                            pe.matmul(bank, ident_b[:, :], mask_t[:, j, cut], start=True, stop=False)
                            depth = 128 if layer == 0 else 97
                            mm = pe.matmul(bank, ks[0:depth, n, blk_j], qs[0:depth, n, cut],
                                           start=False, stop=True)
                        else:
                            pe.wait_ge(s_exp, T - 1)
                            for k, rows_of in enumerate((qs, ks)):
                                bank = ps[:, 2 * (s % 2) + k, :]
                                pe.matmul(bank, ident_b[:, :], mask_t[:, j, cut], start=True, stop=False)
                                mm = pe.matmul(bank, sel[:, 0, :], rows_of[:, n, cut], start=False, stop=True)
                        mm.then_inc(s_score, 1)

                    def weigh(s):
                        n, tt, r = s // TILES, s % TILES, s % RING
                        c, j = tt // BLOCKS, tt % BLOCKS
                        H = CREDIT + 2 * UNIT0[layer] + u * (2 * UNROLL) + 2 * n + c
                        T = tile_value(s)
                        if layer == 0:
                            if j % 2 == 0:
                                pe.wait_ge(s_chfree, CREDIT + u * (TILES // 2 * UNROLL) + s // 2 - 1)
                        elif j == 0:
                            pe.wait_ge(s_accfree, H - (0 if layer == 2 else 1) - 2 * UNITS[0])
                        pe.wait_ge(s_hi, T + 1)
                        pe.wait_ge(s_lo, T + 1)
                        for it in range(IB):
                            if layer == 0:
                                acc = ps[:, 6 + s // 2 % 2, (s % 2 * IB + it) * 33:(s % 2 * IB + it + 1) * 33]
                                opens = s % 2 == 0 and it == 0
                            elif layer == 2:
                                acc = ps[:, 6 + it // 2, it % 2 * width:(it % 2 + 1) * width]
                                opens = j == 0 and it % 2 == 0
                            else:
                                acc = ps[:, 6 + c, it * width:(it + 1) * width]
                                opens = j == 0 and it == 0
                            for h, half in enumerate((phi, plo)):
                                for v in range(3):
                                    at = (j * 3 + v) * width
                                    mm = pe.matmul(acc, half[:, r, it * P:(it + 1) * P], vs[:, n, at:at + width],
                                                   start=opens and h == 0 and v == 0, stop=h == 1 and v == 2,
                                                   skip_group_check=True)
                            if layer == 3 and j == BLOCKS - 1:
                                at_i = c * HALF + it * P
                                for v in range(3):
                                    mm = pe.matmul(acc, empty[:, at_i:at_i + P], zs[:, n, v * 33:(v + 1) * 33],
                                                   start=False, stop=v == 2, skip_group_check=True)
                        mm.then_inc(s_av, 1)

                    for s in range(TILES * UNROLL + LAG):
                        if s < TILES * UNROLL:
                            scores(s)
                            n = s // TILES
                            if layer and not (last and n == UNROLL - 1):
                                for k in range(TILES):
                                    if SHIFT_AT[k] == s % TILES:
                                        if k == 0:
                                            unit_ready((n + 1) % UNROLL, u + (n + 1) // UNROLL)
                                        top_scores((n + 1) % UNROLL, k, SHIFT0[layer] + u * UNROLL + n + 1)
                                if s % TILES == TURN_AT:
                                    turn_shift((n + 1) % UNROLL, SHIFT0[layer] + u * UNROLL + n + 1)
                        if s >= LAG:
                            weigh(s - LAG)

                if layer:
                    unit_ready(0, 0)
                    for k in range(TILES):
                        top_scores(0, k, SHIFT0[layer])
                    turn_shift(0, SHIFT0[layer])
                loop(pe, layer, body)

            node(0)
            pe.wait_ge(s_mask, 2 * BLOCKS)
            heads(0)
            node(1)
            pe.wait_ge(s_krow, 1)
            heads(1)
            node(2)
            pe.wait_ge(s_mask, 4 * BLOCKS)
            pe.wait_ge(s_diag, 4 * BLOCKS)
            heads(2)
            node(3)
            pe.wait_ge(s_diag, 6 * BLOCKS)
            pe.wait_ge(s_ev["row"], ev("row", 3, GRAPHS - 1))
            for c in range(2):
                for j in range(BLOCKS):
                    mm = pe.matmul(ps[:, 4 + c, :], ones_b[:, :], mask_t[:, j, c * HALF:(c + 1) * HALF],
                                   start=j == 0, stop=j == BLOCKS - 1)
            mm.then_inc(s_cnt, 1)
            pe.wait_ge(s_empty, 1)
            heads(3)

        @block.vector
        def _(dve):
            for name in ("y", "eneg", "var", "var0", "xn", "col", "q2", "k2", "row2", "vf", "v"):
                dve.sem_inc(s_ev[name], 1)
            dve.sem_inc(s_shift, SHIFT_CREDIT)
            for s in (s_lo, s_nmax, s_accfree, s_chfree):
                dve.sem_inc(s, CREDIT)
            dve.memset(ones_b[:, :], 1.0).then_inc(s_fill, 1)
            dve.memset(ln2[:, :], LN2).then_inc(s_fill, 1)
            dve.memset(vbuf[:, :, :, :, :], 0.0).then_inc(s_fill, 1)
            dve.memset(v2buf[:, :, :, :], 0.0).then_inc(s_fill, 1)
            dve.memset(vsumb[:, :, :, :], 0.0).then_inc(s_fill, 1)
            dve.wait_ge(s_fill, 5)
            dve.memset(vbuf[:, :, :, 0, 32], 1.0).then_inc(s_fill, 1)
            dve.memset(v2buf[:, :, 0, 128], 1.0).then_inc(s_fill, 1)
            dve.memset(vsumb[:, :, 0, 32], float(BLOCKS)).then_inc(s_fill, 1)
            dve.wait_ge(s_fill, 8)
            dve.wait_ge(s_ident, 5)
            dve.memset(sel[:, :, :].bitcast(F32), 0.0).then_inc(s_sel, 1)
            dve.wait_ge(s_sel, 1)
            dve.memset(sel[0:3, 0, :].bitcast(F32), 1.0).then_inc(s_sel, 1)
            dve.memset(sel[32:34, 1, :].bitcast(F32), 1.0).then_inc(s_sel, 1)
            dve.wait_ge(s_const, 16 * 22)

            def node(stage):
                state = {}

                def link(ins):
                    state["n"] += 1
                    ins.then_inc(state["signal"], 1)
                    dve.wait_ge(state["signal"], state["base"] + state["n"])

                def begin(signal, counts, b):
                    state.update(n=0, signal=signal, base=GRAPHS * sum(counts[:stage]) + b * counts[stage])

                def end(counts):
                    assert state["n"] == counts[stage], (stage, counts, state["n"])

                def row(k):
                    return rows[:, k, :].unsqueeze(1).to_broadcast([P, BLOCKS, F])

                def done(name, b, ins):
                    ins.then_inc(s_ev[name], 1)
                    dve.wait_ge(s_ev[name], ev(name, stage, b))

                def layer_norm(dst, name, b):
                    for it in range(BLOCKS):
                        ins = dve.bn_stats(bns[:, it, :], work[:, it, :])
                    link(ins)
                    dve.sem_inc(s_stats, 1)
                    for it in range(BLOCKS):
                        ins = dve.bn_aggr(mv[:, it, :], bns[:, it, :])
                    link(ins)
                    dve.tensor_scalar(var[:, :], mv[:, :, 1], EPS, None, ALU.add).then_inc(s_ev["var" + name], 1)
                    dve.wait_ge(s_ev["rstd" + name], ev("rstd" + name, stage, b))
                    for it in range(BLOCKS):
                        ins = dve.tensor_scalar(dst[:, it, :], work[:, it, :], mv[:, it, 0:1], rstd[:, it:it + 1],
                                                ALU.subtract, ALU.mult)
                    return ins

                def finish(b, q, h):
                    if stage == 0:
                        return
                    begin(s_chain_a, CHAIN_A, b)
                    w, x = work[:, :, :], xr[:, q, :, :]
                    if stage in (1, 2):
                        dve.wait_ge(s_load[q], load_at(stage, h))
                        dve.wait_ge(s_ev["y_ps"], ev("y_ps", stage, b))
                        y = pf[:, 2 * HALF:4 * HALF].rearrange("p (t f) -> p t f", f=F)
                        done("y", b, dve.tensor_tensor(w, y, row(2 * stage - 1), ALU.add))
                        link(dve.tensor_tensor(w, w, x, ALU.add))
                    if stage == 1:
                        link(layer_norm(work, "0", b))
                        link(dve.tensor_tensor(w, w, row(4), ALU.mult))
                        link(dve.tensor_tensor(w, w, row(5), ALU.add))
                        link(dve.tensor_tensor(w, w, x, ALU.add))
                    if stage in (3, 4):
                        dve.wait_ge(s_load[q], load_at(stage, h))
                        c = cs[:, q, :, :]
                        dve.tensor_scalar(neg[:, :, :], c, 0.0, None, ALU.min).then_inc(s_ev["eneg"], 1)
                        dve.wait_ge(s_ev["eexp"], ev("eexp", stage, b))
                        link(dve.scalar_tensor_tensor(w, c, 0.0, neg[:, :, :], ALU.max, ALU.add))
                        link(dve.scalar_tensor_tensor(w, w, -1.0, x, ALU.add, ALU.add))
                    dve.wait_ge(s_xst[q], xst_before(stage, h))
                    if stage < 4:
                        dve.wait_ge(s_ev["xT_ps"], before("xT_ps", stage, b) - 1)
                    done("xn", b, layer_norm(xn[:, q, :, :], "", b))
                    end(CHAIN_A)

                def project(b, q, h):
                    if stage == 4:
                        return
                    begin(s_chain_b, CHAIN_B, b)
                    dve.wait_ge(s_pst, pst_before(stage, b))
                    if stage < 2:
                        for w, name in enumerate("qk"):
                            dve.wait_ge(s_ev[name], ev(name, stage, b))
                            dve.scalar_tensor_tensor(
                                part[:, w, 1, :], pf[:, (6 - 2 * w) * HALF:(8 - 2 * w) * HALF],
                                bcol[:, 2 * stage + w:2 * stage + w + 1], part[:, w, 0, :].bitcast(F32),
                                ALU.add, ALU.subtract).then_inc(s_ev[name + "2"], 1)
                    else:
                        n = 2 * HEADS[stage]
                        dve.wait_ge(s_ev["row"], ev("row", stage, b))
                        done("col", b, dve.tensor_copy(
                            colp[:, 0:n, :], ps[:, 0, 0:BLOCKS * n].rearrange("p (t r) -> p r t", r=n)))
                        r = full[0:n, 1, :]
                        link(dve.tensor_copy(rowp[0:n, 0, :], r))
                        link(dve.tensor_tensor(rowp[0:n, 1, :], r, rowp[0:n, 0, :].bitcast(F32), ALU.subtract))
                        link(dve.tensor_scalar(r, r, SLOPE, None, ALU.mult))
                        link(dve.tensor_copy(rowp[0:n, 2, :], r))
                        dve.tensor_tensor(rowp[0:n, 3, :], r, rowp[0:n, 2, :].bitcast(F32),
                                          ALU.subtract).then_inc(s_ev["row2"], 1)
                    dve.wait_ge(s_ev["v_ps"], ev("v_ps", stage, b))
                    v = pf[:, 6 * HALF:8 * HALF].rearrange("p (t f) -> p t f", f=F)
                    if stage < 2:
                        done("vf", b, dve.tensor_tensor(vf[:, :, :], v, row(2 * stage), ALU.add))
                    else:
                        done("vf", b, dve.tensor_copy(vf[:, :, :], v))
                    if stage == 3:
                        link(dve.tensor_reduce(vsum[:, :], vf[:, :, :].rearrange("p t f -> p f t"), AX.X, ALU.add))
                        z, zf = (lambda s: vsumb[:, :, s, 0:32]), vsum[:, :].rearrange("p (h d) -> p h d", h=4)
                        link(dve.tensor_copy(z(0), zf))
                        link(dve.tensor_tensor(zf, zf, z(0), ALU.subtract))
                        link(dve.tensor_copy(z(1), zf))
                        link(dve.tensor_tensor(z(2), zf, z(1), ALU.subtract))
                    if stage == 2:
                        piece, f = (lambda s: v2buf[:, :, s, 0:F]), vf[:, :, :]
                    else:
                        piece = lambda s: vbuf[:, :, :, s, 0:32]
                        f = vf[:, :, :].rearrange("p t (h d) -> p h t d", h=4)
                    link(dve.tensor_copy(piece(0), f))
                    link(dve.tensor_tensor(f, f, piece(0), ALU.subtract))
                    link(dve.tensor_copy(piece(1), f))
                    done("v", b, dve.tensor_tensor(piece(2), f, piece(1), ALU.subtract))
                    end(CHAIN_B)

                graphs(dve, finish, project)

            def heads(layer):
                width = WIDTH[layer]
                per = HCHAIN[layer]
                chain0 = sum(HCHAIN[m] * UNITS[m] // UNROLL for m in range(layer))
                state = {}

                def link(ins):
                    state["n"] += 1
                    ins.then_inc(s_hchain, 1)
                    dve.wait_ge(s_hchain, state["base"] + state["n"])

                def find_shift(n):
                    M, z, l = shift[:, 0, :], shift[:, 1, :], shift[:, 2, :]
                    link(dve.tensor_reduce(M, top[:, :, :], AX.X, ALU.max))
                    if layer == 1:
                        dve.tensor_scalar(nshift[:, n % 2, :], M, LEAST, -1.0, ALU.max, ALU.mult
                                          ).then_inc(s_shcol, 1)
                    else:
                        link(dve.tensor_tensor(z, M, cols[:, n, 0, :], ALU.add))
                        link(dve.tensor_scalar(z, z, LEAST, None, ALU.max))
                        link(dve.tensor_scalar(l, z, SLOPE, None, ALU.mult))
                        link(dve.tensor_tensor(l, z, l, ALU.max))
                        dve.tensor_scalar(nshift[:, n % 2, :], l, -1.0, None, ALU.mult).then_inc(s_shcol, 1)
                        dve.tensor_scalar(cols2[:, n, :], cols[:, n, 1, :], SLOPE, None, ALU.mult
                                          ).then_inc(s_cols2, 1)

                def shift_rows(n, U):
                    dve.wait_ge(s_shT, U + 1)
                    dve.tensor_copy(shrow[:, n % 2, :], ps[0:BLOCKS, 4, 0:P]).then_inc(s_shift, 1)

                def take_max(k, U):
                    dve.wait_ge(s_nsc, TILES * U + k + 1)
                    dve.tensor_reduce(top[:, k // 2, k % 2:k % 2 + 1], ps[:, 4 + k % 2, :], AX.X, ALU.max
                                      ).then_inc(s_nmax, 1)
                    if k == TILES - 1:
                        dve.wait_ge(s_nmax, CREDIT + TILES * (U + 1))

                def body(u, last):
                    state["n"] = 0
                    state["base"] = chain0 + HPRE[layer] + u * per

                    def tile_value(s):
                        return CREDIT + TILES * UNIT0[layer] + u * (TILES * UNROLL) + s

                    def settle(s):
                        T, r = tile_value(s), s % RING
                        dve.wait_ge(s_exp, T + 1)
                        p = prob[:, r, :]
                        if layer == 0:
                            dve.tensor_scalar(p, p, CLIP_LO, CLIP_HI, ALU.max, ALU.min).then_inc(s_p, 1)
                        else:
                            dve.tensor_tensor(p, p, prob_b[:, r, :], ALU.max).then_inc(s_p, 1)

                    def low(s):
                        T, r = tile_value(s), s % RING
                        dve.wait_ge(s_hi, T + 1)
                        dve.wait_ge(s_exp, T + 1)
                        dve.wait_ge(s_av, T - RING + 1)
                        dve.tensor_tensor(plo[:, r, :], prob[:, r, :], phi[:, r, :], ALU.subtract
                                          ).then_inc(s_lo, 1)

                    def out_free(n, U):
                        dve.wait_ge(s_outfree, CREDIT + U - 1)

                    def blocks_done(s):
                        n, tt = s // TILES, s % TILES
                        c, j = tt // BLOCKS, tt % BLOCKS
                        acc = ps[:, 6 + s // 2 % 2, 0:2 * IB * 33].rearrange("p (a d) -> p a d", d=33)
                        dve.wait_ge(s_av, tile_value(s) + 1)
                        dve.wait_ge(s_chfree, CREDIT + u * (TILES // 2 * UNROLL) + s // 2)
                        link(dve.reciprocal(rden[:, 0:2 * IB], acc[:, :, 32]))
                        dve.tensor_tensor(blk[:, j - 1:j + 1, :, :].rearrange("p j t d -> p (j t) d"), acc[:, :, 0:32],
                                          rden[:, 0:2 * IB].unsqueeze(2).to_broadcast([P, 2 * IB, 32]),
                                          ALU.mult).then_inc(s_chfree, 1)
                        if j == BLOCKS - 1:
                            dve.wait_ge(s_chfree, CREDIT + u * (TILES // 2 * UNROLL) + s // 2 + 1)
                            U = UNIT0[layer] + u * UNROLL + n
                            if c == 0:
                                out_free(n, U)
                            ins = dve.tensor_reduce(
                                outp[:, n % 2, c * IB * 32:(c + 1) * IB * 32].rearrange("p (t d) -> p t d", d=32),
                                blk[:, :, :, :].rearrange("p j t d -> p t d j"), AX.X, ALU.add)
                            if c == 1:
                                ins.then_inc(s_out, 1)
                                dve.wait_ge(s_out, U + 1)
                            else:
                                link(ins)

                    def half_done(s):
                        n, tt = s // TILES, s % TILES
                        c = tt // BLOCKS
                        U = UNIT0[layer] + u * UNROLL + n
                        dve.wait_ge(s_av, tile_value(s) + 1)
                        if c == 0:
                            out_free(n, U)
                        banks = ((6, 2), (7, 2)) if layer == 2 else ((6 + c, IB),)
                        for m, (bank, blocks) in enumerate(banks):
                            acc = ps[:, bank, 0:blocks * (width + 1)].rearrange("p (t d) -> p t d", d=width + 1)
                            link(dve.tensor_scalar(rden[:, 0:blocks], acc[:, :, width], TINY, None, ALU.max))
                            link(dve.reciprocal(rden[:, 0:blocks], rden[:, 0:blocks]))
                            at = (c * IB + m * 2) * width
                            link(dve.tensor_tensor(
                                outp[:, n % 2, at:at + blocks * width].rearrange("p (t d) -> p t d", d=width),
                                acc[:, :, 0:width],
                                rden[:, 0:blocks].unsqueeze(2).to_broadcast([P, blocks, width]), ALU.mult))
                        dve.sem_inc(s_accfree, 1)
                        if c == 1:
                            dve.sem_inc(s_out, 1)

                    total = TILES * UNROLL
                    for s in range(total + LAG + 2):
                        if s < total:
                            if layer != 1:
                                settle(s)
                            n = s // TILES
                            if layer and not (last and n == UNROLL - 1):
                                U = SHIFT0[layer] + u * UNROLL + n + 1
                                for k in range(TILES):
                                    if SHIFT_AT[k] == s % TILES:
                                        take_max(k, U)
                                        if k == TILES - 1:
                                            find_shift((n + 1) % UNROLL)
                                if s % TILES == TURN_AT:
                                    shift_rows((n + 1) % UNROLL, U)
                        if 1 <= s <= total:
                            low(s - 1)
                        e = s - LAG - 1
                        if 0 <= e < total:
                            if layer == 0 and e % 2:
                                blocks_done(e)
                            if layer and e % BLOCKS == BLOCKS - 1:
                                half_done(e)
                    want = per - (HPRE[layer] if last else 0)
                    assert state["n"] == want, (layer, last, state["n"])

                if layer:
                    state["n"], state["base"] = 0, chain0
                    dve.wait_ge(s_stk[0], stk_at(layer, 0, 0))
                    for k in range(TILES):
                        take_max(k, SHIFT0[layer])
                    find_shift(0)
                    shift_rows(0, SHIFT0[layer])
                    assert state["n"] == HPRE[layer]
                loop(dve, layer, body)

            node(0)
            heads(0)
            node(1)
            heads(1)
            node(2)
            heads(2)
            node(3)
            dve.wait_ge(s_cnt, 1)
            dve.tensor_scalar(empty[:, :], pf[:, 4 * HALF:6 * HALF], -BIG * NODES, None, ALU.is_equal
                              ).then_inc(s_empty, 1)
            heads(3)
            node(4)


_WEIGHTS = ("L0_gnn_Wq", "L0_gnn_Wk", "L0_gnn_Wv", "L0_gnn_Wo", "L1_gnn_wq", "L1_gnn_wk", "L1_gnn_wv", "L1_gnn_wo")
_ROWS = ("L0_gnn_bv", "L0_gnn_bo", "L1_gnn_bv", "L1_gnn_bo", "L0_gnn_gamma", "L0_gnn_beta")
_COLS = ("L0_gnn_bq", "L0_gnn_bk", "L1_gnn_bq", "L1_gnn_bk")


def kernel(**inputs):
    import numpy as np
    import concourse.bacc as bacc
    from concourse import mybir as _mybir
    from concourse.bass_utils import run_bass_kernel_spmd

    a = {n: np.asarray(v) for n, v in inputs.items()}
    arrays = {"x": a["x"], "adj_n": a["adj"], "adj_t": a["adj"].T}
    for n in _WEIGHTS:
        arrays[n] = a[n].T
    for n in _ROWS:
        arrays[n] = np.broadcast_to(a[n], (P, F))
    for n in _COLS:
        arrays[n] = a[n].reshape(F, 1)
    arrays["L2_gnn_W"] = a["L2_gnn_W"]
    arrays["L2_gnn_a"] = a["L2_gnn_a"].reshape(2, F).T
    arrays["L3_gnn_W"] = a["L3_gnn_W"].transpose(1, 0, 2).reshape(F, F)
    side = np.zeros((4, 32, 2, 4), a["L3_gnn_a"].dtype)
    for h in range(4):
        side[h, :, 0, h] = a["L3_gnn_a"][h, :32]
        side[h, :, 1, h] = a["L3_gnn_a"][h, 32:]
    arrays["L3_gnn_a"] = side.reshape(F, 8)
    arrays = {n: np.ascontiguousarray(v) for n, v in arrays.items()}

    nc = bacc.Bacc("TRN2", target_bir_lowering=False, num_devices=1)
    t = {n: nc.dram_tensor("in_" + n, v.shape, _mybir.dt.from_np(v.dtype), kind="ExternalInput").ap()
         for n, v in arrays.items()}
    t["out"] = nc.dram_tensor("out_0", (GRAPHS, NODES, F), F32, kind="ExternalOutput").ap()
    build(nc, t)
    r = run_bass_kernel_spmd(nc, [{"in_" + n: v for n, v in arrays.items()}], core_ids=[0])
    return r.results[0]["out_0"]
```

```python
from contextlib import ExitStack

import concourse.bass as bass
from concourse import mybir

F32 = mybir.dt.float32
F32R = mybir.dt.float32r
BF16 = mybir.dt.bfloat16
F16 = mybir.dt.float16
I32 = mybir.dt.int32
ALU = mybir.AluOpType
ACT = mybir.ActivationFunctionType
AX = mybir.AxisListType

P = 128
GRAPHS, NODES, F = 8, 1024, 128
BLOCKS = NODES // P
HALF = 512
IB = HALF // P
TILES = BLOCKS * 2
LAYERS = 4
HEADS = (4, 4, 1, 4)
WIDTH = tuple(F // h for h in HEADS)
UNITS = tuple(GRAPHS * h for h in HEADS)
UNIT0 = tuple(sum(UNITS[:n]) for n in range(LAYERS))
SHIFT0 = tuple(sum(UNITS[1:n]) for n in range(LAYERS))
BIG = 2.0 ** 100
LEAST = -(2.0 ** 66)
TINY = 2.0 ** -100
LOWEST = -3.0e38
EPS = 1e-5
SLOPE = 0.2
SCALE = 32.0 ** -0.5
LN2 = 0.6931471805599453
CLIP_LO = 2.0 * 4.5399929762484854e-05
CLIP_HI = 2.0 * 22026.465794806718
UNROLL = 4
RING = 4
CREDIT = 32
SHIFT_CREDIT = 1
LAGS = (3, 3, 3, 3)
MAX_AT = 8
TURN_AT = (None, 11, 9, 9)
TURN_BANK = (None, 5, 3, 3)
DVE_LOW = ((3,), (3,), (), ())
V3 = 3 * 33
V3W = 3 * 129
LOADS = (9, 7, 9, 10)
ROWMS = (0, 1, 1, 1)
CHAIN_A = (0, 9, 3, 4, 4)
CHAIN_B = (0, 0, 4, 7)
HCHAIN = (36, 28, 68, 44)
HLEFT = (2, 3, 6, 3)
HPRE = (0, 1, 5, 5)
NODE_LOADS = (1, 5, 5, 2, 5)
PART_STORES = (1, 1, 2, 3)


def build(nc, t):
    with ExitStack() as ctx:
        def sb(name, shape, dt=F32):
            return ctx.enter_context(nc.sbuf_tensor(name, shape, dt))

        def sem(name):
            return ctx.enter_context(nc.semaphore(name))

        ps = ctx.enter_context(nc.psum_tensor("ps", [P, 8, HALF], F32))
        pf = ps[:, :, :].rearrange("p b n -> p (b n)")

        x_d = nc.dram_tensor("x_d", (GRAPHS, P, BLOCKS, F), F32, kind="Internal").ap()
        ctx_d = nc.dram_tensor("ctx_d", (GRAPHS * 4, P, BLOCKS, 32), F32, kind="Internal").ap()
        ctx2_d = nc.dram_tensor("ctx2_d", (GRAPHS, P, BLOCKS * F), F32, kind="Internal").ap()
        q_d = nc.dram_tensor("q_d", (2, GRAPHS * 4 * 32, NODES), F32, kind="Internal").ap()
        k_d = nc.dram_tensor("k_d", (2, GRAPHS * 4 * 32, NODES), F32, kind="Internal").ap()
        v_d = nc.dram_tensor("v_d", (GRAPHS * 4, P, BLOCKS * V3), BF16, kind="Internal").ap()
        v2_d = nc.dram_tensor("v2_d", (GRAPHS, P, BLOCKS * V3W), BF16, kind="Internal").ap()
        row_d = nc.dram_tensor("row_d", (4, GRAPHS * 8, NODES), F32, kind="Internal").ap()
        col_d = nc.dram_tensor("col_d", (GRAPHS * 8, P, BLOCKS), F32, kind="Internal").ap()
        sum_d = nc.dram_tensor("sum_d", (GRAPHS * 4, P, V3), BF16, kind="Internal").ap()

        ident = sb("ident", [P, P])
        ident_b = sb("ident_b", [P, P], BF16)
        ones_b = sb("ones_b", [P, P], BF16)
        expo = sb("expo", [P, BLOCKS])
        ln2 = sb("ln2", [P, 1])
        anti = sb("anti", [P, P], BF16)
        wts = sb("wts", [P, 10, F])
        rows = sb("rows", [P, 6, F])
        bcol = sb("bcol", [P, 4])
        aa = sb("aa", [P, 2, 8])
        mask_n = sb("mask_n", [P, BLOCKS, NODES], BF16)
        mask_t = sb("mask_t", [P, BLOCKS, NODES], BF16)
        empty = sb("empty", [P, NODES], BF16)

        diag = sb("diag", [P, 2, BLOCKS, P], BF16)
        sel = sb("sel", [P, 3, P], F32R)

        xr = sb("xr", [P, 2, BLOCKS, F])
        cs = sb("cs", [P, 2, BLOCKS, F])
        work = sb("work", [P, BLOCKS, F])
        neg = sb("neg", [P, BLOCKS, F])
        xn = sb("xn", [P, 2, BLOCKS, F])
        cT = sb("cT", [P, NODES])
        xT = sb("xT", [P, NODES])
        bns = sb("bns", [P, BLOCKS, 6])
        mv = sb("mv", [P, BLOCKS, 2])
        var = sb("var", [P, BLOCKS])
        rstd = sb("rstd", [P, BLOCKS])
        full = sb("full", [P, 2, NODES])
        part = sb("part", [P, 2, 2, 2, NODES], F32R)
        rowp = part[0:8, :, :, :, :].rearrange("p g a b n -> p g (a b) n")
        vf = sb("vf", [P, BLOCKS, F])
        vbuf = sb("vbuf", [P, 4, BLOCKS, 3, 33], BF16)
        v2buf = sb("v2buf", [P, BLOCKS, 3, 129], BF16)
        vsum = sb("vsum", [P, F])
        vsumb = sb("vsumb", [P, 4, 3, 33], BF16)
        colp = sb("colp", [P, 8, BLOCKS])

        qs = sb("qs", [P, UNROLL, NODES], F32R)
        ks = sb("ks", [P, UNROLL, NODES], F32R)
        vs = sb("vs", [P, UNROLL, BLOCKS * V3W], BF16)
        adj_i = vs[:, :, :].rearrange("p u n -> p (u n)").bitcast(I32)[:, 0:4 * NODES].rearrange(
            "p (k n) -> p k n", n=NODES)
        zs = sb("zs", [P, UNROLL, V3], BF16)
        cols = sb("cols", [P, UNROLL, 2, BLOCKS])
        colx = sb("colx", [P, UNROLL, BLOCKS])
        prob = xr[:, :, :, :].rearrange("p a t f -> p (a t f)").rearrange("p (r n) -> p r n", n=HALF)
        arg = cs[:, :, :, :].rearrange("p a t f -> p (a t f)").rearrange("p (r n) -> p r n", n=HALF)
        phi = cT[:, :].bitcast(F16).rearrange("p (r n) -> p r n", n=HALF)
        plo = xT[:, :].bitcast(BF16).rearrange("p (r n) -> p r n", n=HALF)
        si8 = full[:, 0, :]
        junk = neg[:, :, :].rearrange("p t f -> p (t f)").bitcast(BF16)[:, 0:HALF]
        top = sb("top", [P, BLOCKS, 2])
        shift = sb("shift", [P, 3, BLOCKS])
        nshift = sb("nshift", [P, 2, BLOCKS])
        shrow = sb("shrow", [BLOCKS, 2, P], F32R)
        rden = sb("rden", [P, 8])
        blk = work[:, :, :].rearrange("p j (t d) -> p j t d", d=32)
        outp = xn[:, :, :, :].rearrange("p a t f -> p a (t f)")

        s_const = sem("s_const")
        s_ident = sem("s_ident")
        s_fill = sem("s_fill")
        s_krow = sem("s_krow")
        s_anti = sem("s_anti")
        s_adj = [sem(f"s_adj{n}") for n in range(4)]
        s_mask = sem("s_mask")
        s_diag = sem("s_diag")
        s_zero = sem("s_zero")
        s_sel = sem("s_sel")
        s_cnt = sem("s_cnt")
        s_empty = sem("s_empty")
        s_load = [sem("s_load0"), sem("s_load1")]
        s_xst = [sem("s_xst0"), sem("s_xst1")]
        s_pst = sem("s_pst")
        s_rst = [sem("s_rst0"), sem("s_rst1")]
        s_chain_a = sem("s_chain_a")
        s_chain_b = sem("s_chain_b")
        s_carry = sem("s_carry")
        s_hchain = sem("s_hchain")
        s_stk = [sem(f"s_stk{n}") for n in range(UNROLL)]
        s_rowm = [sem(f"s_rowm{n}") for n in range(UNROLL)]
        s_colx = sem("s_colx")
        s_si = sem("s_si")
        s_si8 = sem("s_si8")
        s_score = sem("s_score")
        s_exp = sem("s_exp")
        s_p = sem("s_p")
        s_hi = sem("s_hi")
        s_lo = sem("s_lo")
        s_lo_dve = sem("s_lo_dve")
        s_av = sem("s_av")
        s_accfree = sem("s_accfree")
        s_chfree = sem("s_chfree")
        s_nsc = sem("s_nsc")
        s_nmax = sem("s_nmax")
        s_shcol = sem("s_shcol")
        s_shT = sem("s_shT")
        s_shift = sem("s_shift")
        s_out = sem("s_out")
        s_ctx = [sem("s_ctx0"), sem("s_ctx1")]
        EVENTS = {
            "cT_ps": (1, 2),
            "cT": (1, 2),
            "y_ps": (1, 2),
            "y": (1, 2),
            "eneg": (3, 4),
            "eexp": (3, 4),
            "var": (1, 2, 3, 4),
            "rstd": (1, 2, 3, 4),
            "var0": (1,),
            "rstd0": (1,),
            "xn": (1, 2, 3, 4),
            "xT_ps": (0, 1, 2, 3),
            "xT": (0, 1, 2, 3),
            "q_ps": (0, 1),
            "k_ps": (0, 1),
            "w_ps": (2, 3),
            "v_ps": (0, 1, 2, 3),
            "row_ps": (2, 3),
            "q": (0, 1),
            "k": (0, 1),
            "w": (2, 3),
            "row": (2, 3),
            "col": (2, 3),
            "q2": (0, 1),
            "k2": (0, 1),
            "row2": (2, 3),
            "vf": (0, 1, 2, 3),
            "vsum": (3,),
            "v0": (0, 1, 2, 3),
            "vr": (0, 1, 2, 3),
            "v1": (0, 1, 2, 3),
            "v": (0, 1, 2, 3),
            "vs": (3,),
        }
        s_ev = {name: sem("s_" + name) for name in EVENTS}

        def ev(name, stage, b):
            assert stage in EVENTS[name]
            return 2 + GRAPHS * EVENTS[name].index(stage) + b

        def before(name, stage, b):
            if stage in EVENTS[name]:
                return 1 + GRAPHS * EVENTS[name].index(stage) + b
            return 1 + GRAPHS * sum(s < stage for s in EVENTS[name])

        def load_at(stage, h):
            return 16 * (GRAPHS // 2) * sum(NODE_LOADS[:stage]) + (h + 1) * (16 * NODE_LOADS[stage])

        def xst_before(stage, h):
            return 16 + 16 * (GRAPHS // 2) * max(stage - 1, 0) + h * 16

        def pst_before(stage, b):
            return 16 + 16 * GRAPHS * sum(PART_STORES[:stage]) + b * (16 * PART_STORES[stage])

        def rst_before(stage, h):
            return 16 + 16 * 4 * (GRAPHS // 2) * stage + h * (16 * 4)

        def stk_at(layer, n, u):
            return 16 * sum(LOADS[m] * UNITS[m] // UNROLL for m in range(layer)) + (u + 1) * (16 * LOADS[layer])

        def rowm_at(layer, n, u):
            return 16 * sum(ROWMS[m] * UNITS[m] // UNROLL for m in range(layer)) + (u + 1) * (16 * ROWMS[layer])

        def low_done(layer, u, s):
            own = DVE_LOW[layer]
            mine = s % RING in own
            slots = [r for r in range(RING) if (r in own) == mine]
            before_layer = sum(UNITS[m] * (TILES // RING) * (len(DVE_LOW[m]) if mine else RING - len(DVE_LOW[m]))
                               for m in range(layer))
            done = s // RING * len(slots) + sum(r <= s % RING for r in slots)
            per_body = UNROLL * (TILES // RING) * len(slots)
            return (s_lo_dve if mine else s_lo), CREDIT + before_layer + u * per_body + done

        def wait_low(eng, layer, u, s):
            signal, value = low_done(layer, u, s)
            eng.wait_ge(signal, value)

        def take_low(eng, layer, u, s):
            T, r = CREDIT + TILES * UNIT0[layer] + u * (TILES * UNROLL) + s, s % RING
            eng.wait_ge(s_hi, T + 1)
            eng.wait_ge(s_exp, T + 1)
            eng.wait_ge(s_av, T - RING + 1)
            eng.tensor_tensor(plo[:, r, :], prob[:, r, :], phi[:, r, :], ALU.subtract
                              ).then_inc(low_done(layer, u, s)[0], 1)

        def stored_before(layer, u, n):
            return 16 + 8 * UNIT0[layer] + u * (8 * UNROLL) + n // 2 * 16

        def loop(eng, layer, body):
            n = UNITS[layer] // UNROLL
            body(0, True, False)
            if n > 2:
                with eng.Fori(1, n - 1) as u:
                    body(u, False, False)
            body(n - 1, False, True)

        def graphs(eng, finish, project):
            finish(0, 0, 0)
            with eng.Fori(0, GRAPHS // 2 - 1) as h:
                finish(h * 2 + 1, 1, h)
                project(h * 2, 0, h)
                finish(h * 2 + 2, 0, h + 1)
                project(h * 2 + 1, 1, h)
            h = GRAPHS // 2 - 1
            finish(2 * h + 1, 1, h)
            project(2 * h, 0, h)
            project(2 * h + 1, 1, h)

        def v_parts(stage):
            if stage == 2:
                return (lambda s: v2buf[:, :, s, 0:F]), vf[:, :, :]
            return (lambda s: vbuf[:, :, :, s, 0:32]), vf[:, :, :].rearrange("p t (h d) -> p h t d", h=4)

        x_in = t["x"].rearrange("b (t p) f -> b p t f", p=P)
        x_out = t["out"].rearrange("b (t p) f -> b p t f", p=P)

        def one(ap, i):
            return ap[bass.ds(i, 1)]

        block = ctx.enter_context(nc.Block())

        @block.sync
        def _(sp):
            for k, name in enumerate(("L0_gnn_Wq", "L0_gnn_Wk", "L0_gnn_Wv", "L0_gnn_Wo",
                                      "L1_gnn_wq", "L1_gnn_wk", "L1_gnn_wv", "L1_gnn_wo",
                                      "L2_gnn_W", "L3_gnn_W")):
                sp.dma_start(wts[:, k, :], t[name]).then_inc(s_const, 16)
            for k, name in enumerate(("L0_gnn_bv", "L0_gnn_bo", "L1_gnn_bv", "L1_gnn_bo",
                                      "L0_gnn_gamma", "L0_gnn_beta")):
                sp.dma_start(rows[:, k, :], t[name]).then_inc(s_const, 16)
            for k, name in enumerate(("L0_gnn_bq", "L0_gnn_bk", "L1_gnn_bq", "L1_gnn_bk")):
                sp.dma_start(bcol[:, k:k + 1], t[name]).then_inc(s_const, 16)
            sp.dma_start(aa[:, 0, 0:2], t["L2_gnn_a"]).then_inc(s_const, 16)
            sp.dma_start(aa[:, 1, :], t["L3_gnn_a"]).then_inc(s_const, 16)

            def load_graph(stage, b, q, h):
                src = one(x_in if stage < 2 else x_d, b).rearrange("a p t f -> (a p) t f")
                if stage == 0:
                    if not (isinstance(b, int) and b < 2):
                        sp.wait_ge(s_ev["xT_ps"], ev("xT_ps", stage, b) - 2)
                    sp.dma_start(xn[:, q, :, :], src).then_inc(s_load[q], 16)
                    return
                sp.dma_start(xr[:, q, :, :], src).then_inc(s_load[q], 16)
                if stage == 3:
                    sp.dma_start(cs[:, q, :, :].rearrange("p t f -> p (t f)"),
                                 one(ctx2_d, b).rearrange("a p n -> (a p) n")).then_inc(s_load[q], 16)
                else:
                    for k in range(4):
                        sp.dma_start(cs[:, q, :, 32 * k:32 * k + 32],
                                     one(ctx_d, b * 4 + k).rearrange("a p t f -> (a p) t f")
                                     ).then_inc(s_load[q], 16)

            def node(stage):
                def finish(b, q, h):
                    if isinstance(b, int) and b == 0:
                        load_graph(stage, 0, 0, 0)
                        load_graph(stage, 1, 1, 0)
                    if stage:
                        sp.wait_ge(s_ev["xn"], ev("xn", stage, b))
                        dst = x_out if stage == 4 else x_d
                        sp.dma_start(one(dst, b).rearrange("a p t f -> (a p) t f"), xn[:, q, :, :]
                                     ).then_inc(s_xst[q], 16)
                    load_graph(stage, b + 2, q, h + 1)

                def project(b, q, h):
                    if stage == 4:
                        return
                    if stage < 2:
                        for w, (name, dst) in enumerate((("q2", q_d), ("k2", k_d))):
                            sp.wait_ge(s_ev[name], ev(name, stage, b))
                            for s in range(2):
                                sp.dma_start(dst[s, bass.ds(b * P, P)], part[:, q, w, s, :].bitcast(F32)
                                             ).then_inc(s_rst[q], 16)
                    else:
                        n = 2 * HEADS[stage]
                        sp.wait_ge(s_ev["row2"], ev("row2", stage, b))
                        for kind in range(4):
                            sp.dma_start(row_d[kind, bass.ds(b * 8, n)], rowp[0:n, q, kind, :].bitcast(F32)
                                         ).then_inc(s_rst[q], 16)
                        sp.dma_start(col_d[bass.ds(b * 8, n)].rearrange("r p t -> p r t"), colp[:, 0:n, :]
                                     ).then_inc(s_pst, 16)
                    sp.wait_ge(s_ev["v"], ev("v", stage, b))
                    if stage == 2:
                        sp.dma_start(one(v2_d, b).rearrange("a p n -> (a p) n"),
                                     v2buf[:, :, :, :].rearrange("p t s d -> p (t s d)")).then_inc(s_pst, 16)
                    else:
                        sp.dma_start(v_d[bass.ds(b * 4, 4)].rearrange("h p n -> p h n"),
                                     vbuf[:, :, :, :, :].rearrange("p h t s d -> p h (t s d)")
                                     ).then_inc(s_pst, 16)
                    if stage == 3:
                        sp.wait_ge(s_ev["vs"], ev("vs", stage, b))
                        sp.dma_start(sum_d[bass.ds(b * 4, 4)].rearrange("h p n -> p h n"),
                                     vsumb[:, :, :, :].rearrange("p h s d -> p h (s d)")).then_inc(s_pst, 16)

                finish(0, 0, 0)
                with sp.Fori(0, GRAPHS // 2 - 2) as h:
                    finish(h * 2 + 1, 1, h)
                    project(h * 2, 0, h)
                    finish(h * 2 + 2, 0, h + 1)
                    project(h * 2 + 1, 1, h)
                h = GRAPHS // 2 - 2
                finish(2 * h + 1, 1, h)
                project(2 * h, 0, h)
                store_last(stage, 2 * h + 2, 0)
                project(2 * h + 1, 1, h)
                store_last(stage, 2 * h + 3, 1)
                project(2 * h + 2, 0, h + 1)
                project(2 * h + 3, 1, h + 1)
                if stage:
                    for q in range(2):
                        sp.wait_ge(s_xst[q], xst_before(stage, GRAPHS // 2))
                if stage < 4:
                    sp.wait_ge(s_pst, pst_before(stage, GRAPHS))
                    for q in range(2):
                        sp.wait_ge(s_rst[q], rst_before(stage, GRAPHS // 2))

            def store_last(stage, b, q):
                if stage:
                    sp.wait_ge(s_ev["xn"], ev("xn", stage, b))
                    dst = x_out if stage == 4 else x_d
                    sp.dma_start(one(dst, b).rearrange("a p t f -> (a p) t f"), xn[:, q, :, :]
                                 ).then_inc(s_xst[q], 16)

            def load_unit(layer, u, m):
                g, n = u * UNROLL + m, m % UNROLL
                count = 0

                def go(dst, src):
                    nonlocal count
                    count += 1
                    sp.dma_start(dst, src).then_inc(s_stk[n], 16)

                if layer < 2:
                    for r, (a, c) in enumerate(((0, 0), (0, 1), (1, 0), (1, 1))[:4 - layer]):
                        go(qs[32 * r:32 * r + 32, n, :].bitcast(F32), q_d[a, bass.ds(g * 32, 32)])
                        go(ks[32 * r:32 * r + 32, n, :].bitcast(F32), k_d[c, bass.ds(g * 32, 32)])
                    go(vs[:, n, 0:BLOCKS * V3], one(v_d, g).rearrange("a p n -> (a p) n"))
                else:
                    heads = HEADS[layer]
                    r = g * 8 if heads == 1 else (u + m // UNROLL) * 8 + n
                    for k in range(2):
                        go(qs[k:k + 1, n, :].bitcast(F32), row_d[k, bass.ds(r, 1)])
                        go(qs[32 + k:33 + k, n, :].bitcast(F32), row_d[k, bass.ds(r + heads, 1)])
                        go(qs[64 + k:65 + k, n, :].bitcast(F32), row_d[2 + k, bass.ds(r, 1)])
                    for k in range(2):
                        go(cols[:, n, k, :], one(col_d, r + k * heads).rearrange("a p t -> (a p) t"))
                    if layer == 2:
                        go(vs[:, n, :], one(v2_d, g).rearrange("a p n -> (a p) n"))
                    else:
                        go(vs[:, n, 0:BLOCKS * V3], one(v_d, g).rearrange("a p n -> (a p) n"))
                        go(zs[:, n, :], one(sum_d, g).rearrange("a p n -> (a p) n"))
                assert count == LOADS[layer]

            def place_shift(layer, g, n):
                sp.wait_ge(s_shift, SHIFT_CREDIT + SHIFT0[layer] + g + 1)
                sp.dma_start(qs[96:97, n, :].bitcast(F32).rearrange("a (t p) -> a t p", p=P),
                             shrow[:, n % 2, :].bitcast(F32)).then_inc(s_rowm[n], 16)

            def store_output(layer, g, n):
                sp.wait_ge(s_out, UNIT0[layer] + g + 1)
                if layer == 2:
                    sp.dma_start(one(ctx2_d, g).rearrange("a p n -> (a p) n"), outp[:, n % 2, :]
                                 ).then_inc(s_ctx[n % 2], 16)
                else:
                    sp.dma_start(one(ctx_d, g).rearrange("a p t f -> (a p) (t f)"),
                                 outp[:, n % 2, 0:BLOCKS * 32]).then_inc(s_ctx[n % 2], 16)

            def heads(layer):
                if layer == 2:
                    sp.wait_ge(s_zero, 1)
                if layer in (0, 2):
                    sp.wait_ge(s_mask, (layer + 2) * BLOCKS)
                for n in range(3):
                    load_unit(layer, 0, n)
                if layer:
                    place_shift(layer, 0, 0)

                def body(u, first, last):
                    for n in range(UNROLL):
                        g = u * UNROLL + n
                        if n or not first:
                            store_output(layer, g - 1, (n - 1) % UNROLL)
                        if layer and not (last and n == UNROLL - 1):
                            place_shift(layer, g + 1, (n + 1) % UNROLL)
                        if not (last and n):
                            sp.wait_ge(s_av, CREDIT + TILES * UNIT0[layer] + g * TILES)
                            load_unit(layer, u, n + 3)

                loop(sp, layer, body)
                store_output(layer, UNITS[layer] - 1, UNROLL - 1)
                for q in range(2):
                    sp.wait_ge(s_ctx[q], stored_before(layer + 1, 0, 0) if layer + 1 < LAYERS else
                               16 + 8 * (UNIT0[layer] + UNITS[layer]))

            node(0)
            heads(0)
            node(1)
            heads(1)
            node(2)
            heads(2)
            node(3)
            heads(3)
            node(4)

        @block.gpsimd
        def _(pool):
            pool.memset(ident[:, :], 0.0).then_inc(s_ident, 1)
            pool.memset(ident_b[:, :], 0.0).then_inc(s_ident, 1)
            pool.memset(expo[:, :], -0.5).then_inc(s_ident, 1)
            pool.wait_ge(s_ident, 3)
            for m in (ident, ident_b):
                pool.affine_select(out=m[:, :], in_=m[:, :], compare_op=ALU.not_equal, fill=1.0, base=0,
                                   pattern=[[-1, P]], channel_multiplier=1).then_inc(s_ident, 1)
            pool.memset(anti[:, :], 1.0).then_inc(s_anti, 1)
            pool.wait_ge(s_anti, 1)
            pool.affine_select(out=anti[:, :], in_=anti[:, :], compare_op=ALU.not_equal, fill=0.0, base=0,
                               pattern=[[-1, P]], channel_multiplier=1).then_inc(s_anti, 1)
            pool.sem_inc(s_lo, CREDIT)
            for s in (*s_xst, s_pst, *s_rst, *s_ctx):
                pool.sem_inc(s, 16)
            for name in ("rstd", "rstd0", "vr", "v"):
                pool.sem_inc(s_ev[name], 1)

            adj_blocks = [t[name].rearrange("(b p) n -> b p n", p=P) for name in ("adj_t", "adj_n")]

            def load_adj(b, q):
                for k in range(2):
                    pool.dma_start(adj_i[:, 2 * q + k, :], one(adj_blocks[k], b).rearrange("a p n -> (a p) n")
                                   ).then_inc(s_adj[2 * q + k], 16)

            def diagonal(k):
                d = (mask_n if k % 2 else mask_t)[:, k // 2, k // 2 * P:(k // 2 + 1) * P]
                keep = diag[:, k % 2, k // 2, :]
                pool.tensor_copy(keep, d).then_inc(s_diag, 1)
                pool.wait_ge(s_diag, 2 * k + 1)
                pool.tensor_tensor(d, keep, anti[:, :], ALU.mult).then_inc(s_diag, 1)
                pool.wait_ge(s_diag, 2 * k + 2)

            def power(stage, name, b):
                pool.wait_ge(s_ev["var" + name], ev("var" + name, stage, b))
                pool.tensor_tensor(rstd[:, :], var[:, :], expo[:, :], ALU.pow).then_inc(s_ev["rstd" + name], 1)

            def node(stage):
                def finish(b, q, h):
                    if stage == 1:
                        power(stage, "0", b)
                    if stage:
                        power(stage, "", b)

                def project(b, q, h):
                    if stage == 4:
                        return
                    piece, f = v_parts(stage)
                    if stage == 3:
                        pool.wait_ge(s_ev["vsum"], ev("vsum", stage, b))
                    pool.wait_ge(s_ev["v0"], ev("v0", stage, b))
                    pool.tensor_tensor(f, f, piece(0), ALU.subtract).then_inc(s_ev["vr"], 1)
                    pool.wait_ge(s_ev["v1"], ev("v1", stage, b))
                    pool.wait_ge(s_pst, pst_before(stage, b))
                    pool.wait_ge(s_ev["vr"], ev("vr", stage, b))
                    pool.tensor_tensor(piece(2), f, piece(1), ALU.subtract).then_inc(s_ev["v"], 1)
                    pool.wait_ge(s_ev["v"], ev("v", stage, b))
                    if stage in (0, 2):
                        pool.wait_ge(s_mask, (GRAPHS * stage + 2) + b * 2)
                        if not isinstance(b, int) or b < GRAPHS - 2:
                            load_adj(b + 2, q)
                    if stage == 2:
                        for k in range(2):
                            diagonal(2 * b + k)

                if stage in (0, 2):
                    load_adj(0, 0)
                    load_adj(1, 1)
                if stage != 2:
                    graphs(pool, finish, project)
                    return
                finish(0, 0, 0)
                for b in range(GRAPHS):
                    if b + 1 < GRAPHS:
                        finish(b + 1, (b + 1) % 2, (b + 1) // 2)
                    project(b, b % 2, b // 2)

            def heads(layer):
                def body(u, first, last):
                    for s in range(TILES * UNROLL):
                        if s % RING not in DVE_LOW[layer]:
                            take_low(pool, layer, u, s)

                loop(pool, layer, body)
                wait_low(pool, layer, UNITS[layer] // UNROLL, -1 - len(DVE_LOW[layer]))
                pool.wait_ge(s_av, CREDIT + TILES * (UNIT0[layer] + UNITS[layer]))

            node(0)
            heads(0)
            pool.memset(ks[96:97, :, :].bitcast(F32), 1.0).then_inc(s_krow, 1)
            pool.wait_ge(s_krow, 1)
            node(1)
            heads(1)
            pool.memset(qs[:, :, :].bitcast(F32), 0.0).then_inc(s_zero, 1)
            node(2)
            heads(2)
            for k in range(2 * BLOCKS):
                d = (mask_n if k % 2 else mask_t)[:, k // 2, k // 2 * P:(k // 2 + 1) * P]
                pool.tensor_copy(d, diag[:, k % 2, k // 2, :]).then_inc(s_diag, 1)
            node(3)
            heads(3)
            node(4)

        @block.scalar
        def _(act):
            for name in ("cT", "eexp", "xT", "q", "k", "w", "row", "v0", "v1"):
                act.sem_inc(s_ev[name], 1)
            act.sem_inc(s_exp, CREDIT)
            act.sem_inc(s_hi, CREDIT)
            act.sem_inc(s_si8, CREDIT)
            act.wait_ge(s_const, 16 * 22)

            def node(stage):
                def finish(b, q, h):
                    if stage in (1, 2):
                        act.wait_ge(s_ev["cT_ps"], ev("cT_ps", stage, b))
                        act.wait_ge(s_ev["y_ps"], before("y_ps", stage, b))
                        act.activation(cT[:, :], pf[:, 0:NODES], ACT.Copy).then_inc(s_ev["cT"], 1)
                    if stage in (3, 4):
                        act.wait_ge(s_ev["eneg"], ev("eneg", stage, b))
                        act.activation(neg[:, :, :], neg[:, :, :], ACT.Exp).then_inc(s_ev["eexp"], 1)

                def project(b, q, h):
                    if stage == 4:
                        return
                    act.wait_ge(s_ev["xT_ps"], ev("xT_ps", stage, b))
                    act.wait_ge(s_ev["v_ps"], before("v_ps", stage, b))
                    act.activation(xT[:, :], pf[:, 4 * HALF:6 * HALF], ACT.Copy).then_inc(s_ev["xT"], 1)
                    if stage < 2:
                        act.wait_ge(s_rst[q], rst_before(stage, h))
                        for w, name in enumerate("qk"):
                            act.wait_ge(s_ev[name + "_ps"], ev(name + "_ps", stage, b))
                            act.activation(part[:, q, w, 0, :], pf[:, (6 - 2 * w) * HALF:(8 - 2 * w) * HALF],
                                           ACT.Identity, bias=bcol[:, 2 * stage + w:2 * stage + w + 1]
                                           ).then_inc(s_ev[name], 1)
                        split_v(b)
                        return
                    n = 2 * HEADS[stage]
                    act.wait_ge(s_ev["w_ps"], ev("w_ps", stage, b))
                    act.wait_ge(s_ev["row_ps"], before("row_ps", stage, b))
                    act.activation(full[:, 0, :], pf[:, 6 * HALF:8 * HALF], ACT.Copy).then_inc(s_ev["w"], 1)
                    act.wait_ge(s_ev["row_ps"], ev("row_ps", stage, b))
                    act.wait_ge(s_ev["row2"], before("row2", stage, b))
                    act.activation(full[0:n, 1, :], pf[0:n, 4 * HALF:6 * HALF], ACT.Copy).then_inc(s_ev["row"], 1)
                    split_v(b)

                def split_v(b):
                    piece, f = v_parts(stage)
                    act.wait_ge(s_ev["vf"], ev("vf", stage, b))
                    act.wait_ge(s_pst, pst_before(stage, b))
                    act.activation(piece(0), f, ACT.Copy).then_inc(s_ev["v0"], 1)
                    act.wait_ge(s_ev["vr"], ev("vr", stage, b))
                    act.activation(piece(1), f, ACT.Copy).then_inc(s_ev["v1"], 1)

                graphs(act, finish, project)

            def heads(layer):
                def body(u, first, last):
                    def tile_value(s):
                        return CREDIT + TILES * UNIT0[layer] + u * (TILES * UNROLL) + s

                    def p_at(s):
                        return tile_value(s) - CREDIT + 1 - (TILES * UNITS[1] if layer > 1 else 0)

                    def scale_i(s):
                        n, c = s // TILES, s // BLOCKS % 2
                        act.wait_ge(s_si, 2 * (UNIT0[layer] - UNIT0[2]) + u * (2 * UNROLL) + s // BLOCKS + 1)
                        act.wait_ge(s_p, p_at(s - BLOCKS - 1))
                        act.activation(si8[:, c * HALF:(c + 1) * HALF], ps[:, 2 + c, :], ACT.Copy,
                                       scale=1.0 - SLOPE).then_inc(s_si8, 1)

                    def exps(s):
                        T, r = tile_value(s), s % RING
                        src, more = ps[:, r, :], dict(scale=SCALE)
                        if layer < 2:
                            act.wait_ge(s_score, T - CREDIT + 1)
                        else:
                            act.wait_ge(s_p, p_at(s))
                            n, j = s // TILES, s % BLOCKS
                            src, more = arg[:, r, :], dict(bias=cols[:, n, 1, j:j + 1])
                        wait_low(act, layer, u, s - RING)
                        if layer == 0:
                            act.activation(prob[:, r, :], src, ACT.Exp, scale=SCALE, bias=ln2[:, 0:1]
                                           ).then_inc(s_exp, 1)
                            return
                        act.activation(prob[:, r, :], src, ACT.Exp, **more).then_inc(s_exp, 1)
                        act.wait_ge(s_av, T - RING + 1)
                        act.activation(phi[:, r, :], src, ACT.Exp, **more).then_inc(s_hi, 1)

                    def high(s):
                        T, r = tile_value(s), s % RING
                        act.wait_ge(s_p, p_at(s))
                        act.wait_ge(s_av, T - RING + 1)
                        act.activation(phi[:, r, :], prob[:, r, :], ACT.Copy).then_inc(s_hi, 1)

                    total = TILES * UNROLL
                    for s in range(total + last):
                        if s < total:
                            if layer > 1 and s == 0:
                                scale_i(0)
                            if layer > 1 and s % BLOCKS == BLOCKS - 1 and s + 1 < total:
                                scale_i(s + 1)
                            exps(s)
                        if layer == 0 and (s or not first):
                            high(s - 1)

                loop(act, layer, body)

            act.wait_ge(s_fill, 8)
            node(0)
            heads(0)
            node(1)
            heads(1)
            node(2)
            heads(2)
            node(3)
            heads(3)
            node(4)

        @block.tensor
        def _(pe):
            for name in ("cT_ps", "y_ps", "xT_ps", "q_ps", "k_ps", "w_ps", "v_ps", "row_ps"):
                pe.sem_inc(s_ev[name], 1)
            pe.sem_inc(s_av, CREDIT)
            pe.wait_ge(s_const, 16 * 22)
            pe.wait_ge(s_ident, 5)
            pe.wait_ge(s_fill, 8)
            pe.wait_ge(s_sel, 5)

            def node(stage):
                def finish(b, q, h):
                    if stage not in (1, 2):
                        return
                    wo = wts[:, 4 * (stage - 1) + 3, :]
                    pe.wait_ge(s_load[q], load_at(stage, h))
                    if stage == 2:
                        pe.wait_ge(s_ev["col"], before("col", stage, b) - 1)
                    for it in range(BLOCKS):
                        mm = pe.transpose(pf[:, it * P:(it + 1) * P], cs[:, q, it, :], ident[:, :])
                    mm.then_inc(s_ev["cT_ps"], 1)
                    pe.wait_ge(s_ev["cT"], ev("cT", stage, b))
                    pe.wait_ge(s_ev["y"], before("y", stage, b))
                    pe.wait_ge(s_ev["vf"], before("vf", stage, b) - 1)
                    for it in range(BLOCKS):
                        mm = pe.matmul(pf[:, 2 * HALF + it * P:2 * HALF + (it + 1) * P],
                                       cT[:, it * P:(it + 1) * P], wo, start=True, stop=True)
                    mm.then_inc(s_ev["y_ps"], 1)

                def project(b, q, h):
                    if stage < 2:
                        pe.wait_ge(s_ev["k2"], before("k2", stage, b))
                    else:
                        pe.wait_ge(s_ev["row"], before("row", stage, b))
                    if stage == 0:
                        pe.wait_ge(s_load[q], load_at(stage, h))
                    else:
                        pe.wait_ge(s_ev["xn"], ev("xn", stage, b))
                    for it in range(BLOCKS):
                        mm = pe.transpose(pf[:, 4 * HALF + it * P:4 * HALF + (it + 1) * P], xn[:, q, it, :],
                                          ident[:, :])
                    mm.then_inc(s_ev["xT_ps"], 1)
                    pe.wait_ge(s_ev["xT"], ev("xT", stage, b))
                    if stage < 2:
                        for w, name in enumerate("qk"):
                            if w == 0:
                                pe.wait_ge(s_ev["q2"], before("q2", stage, b))
                            for c in range(2):
                                mm = pe.matmul(ps[:, 6 - 2 * w + c, :], wts[:, 4 * stage + w, :],
                                               xT[:, c * HALF:(c + 1) * HALF], start=True, stop=True)
                            mm.then_inc(s_ev[name + "_ps"], 1)
                        project_v(b, wts[:, 4 * stage + 2, :])
                        return
                    n, wv = 2 * HEADS[stage], wts[:, 6 + stage, :]
                    a = aa[:, stage - 2, 0:n]
                    pe.wait_ge(s_ev["w"], before("w", stage, b))
                    for c in range(2):
                        mm = pe.matmul(ps[:, 6 + c, :], wv, xT[:, c * HALF:(c + 1) * HALF],
                                       start=True, stop=True)
                    mm.then_inc(s_ev["w_ps"], 1)
                    project_v(b, wv)
                    pe.wait_ge(s_ev["w"], ev("w", stage, b))
                    pe.wait_ge(s_ev["col"], before("col", stage, b))
                    for c in range(2):
                        pe.matmul(ps[0:n, 4 + c, :], a, full[:, 0, c * HALF:(c + 1) * HALF],
                                  start=True, stop=True)
                    for it in range(BLOCKS):
                        mm = pe.matmul(ps[:, 0, it * n:(it + 1) * n], full[:, 0, it * P:(it + 1) * P], a,
                                       start=True, stop=True)
                    mm.then_inc(s_ev["row_ps"], 1)

                def project_v(b, wv):
                    pe.wait_ge(s_ev["vf"], before("vf", stage, b))
                    if stage in (1, 2):
                        latest = isinstance(b, int) and b == GRAPHS - 1
                        pe.wait_ge(s_ev["y"], ev("y", stage, b) + (0 if latest else 1))
                    for it in range(BLOCKS):
                        mm = pe.matmul(pf[:, 2 * HALF + it * P:2 * HALF + (it + 1) * P],
                                       xT[:, it * P:(it + 1) * P], wv, start=True, stop=True)
                    mm.then_inc(s_ev["v_ps"], 1)

                graphs(pe, finish, project)

            def heads(layer):
                width = WIDTH[layer] + 1

                def unit_ready(n, u):
                    pe.wait_ge(s_stk[n], stk_at(layer, n, u))

                def spread(n, c, U):
                    pe.wait_ge(s_nmax, CREDIT + TILES * U - (0 if c else BLOCKS))
                    pe.matmul(ps[:, 4 + c, :], sel[0:64, 1, :], qs[0:64, n, c * HALF:(c + 1) * HALF],
                              start=True, stop=True).then_inc(s_nsc, 1)

                def top_scores(n, k, U):
                    it, c = k // 2, k % 2
                    bank = ps[:, 4 + k % 2, :]
                    pe.wait_ge(s_nmax, CREDIT + TILES * U + k - 1)
                    if k == 3:
                        pe.wait_ge(s_shift, SHIFT_CREDIT + U)
                    cut = slice(c * HALF, (c + 1) * HALF)
                    pe.matmul(bank, qs[0:96, n, it * P:(it + 1) * P], ks[0:96, n, cut],
                              start=True, stop=True).then_inc(s_nsc, 1)

                def turn_shift(n, U, taken=0):
                    pe.wait_ge(s_shcol, U + 1)
                    if layer == 1:
                        pe.wait_ge(s_nmax, CREDIT + TILES * (U + 1) + taken)
                    if layer > 1:
                        pe.wait_ge(s_si8, CREDIT + 2 * (U - SHIFT0[2]))
                    pe.transpose(ps[0:BLOCKS, TURN_BANK[layer], 0:P], nshift[:, n % 2, :], ident[:, :]).then_inc(s_shT, 1)

                def body(u, first, last):
                    def tile_value(s):
                        return CREDIT + TILES * UNIT0[layer] + u * (TILES * UNROLL) + s

                    def scores(s):
                        n, tt = s // TILES, s % TILES
                        c, j = tt // BLOCKS, tt % BLOCKS
                        cut, blk_j = slice(c * HALF, (c + 1) * HALF), slice(j * P, (j + 1) * P)
                        T = tile_value(s)
                        if tt == 0:
                            unit_ready(n, u)
                            if layer:
                                pe.wait_ge(s_rowm[n], rowm_at(layer, n, u))
                        if layer < 2:
                            bank = ps[:, s % RING, :]
                            pe.wait_ge(s_exp if layer == 0 else s_hi, T - RING + 1)
                            pe.matmul(bank, ident_b[:, :], mask_t[:, j, cut], start=True, stop=False)
                            depth = 128 if layer == 0 else 97
                            mm = pe.matmul(bank, ks[0:depth, n, blk_j], qs[0:depth, n, cut],
                                           start=False, stop=True)
                        else:
                            pe.wait_ge(s_p, T - 1 - CREDIT - TILES * UNITS[1])
                            bank = ps[:, s % 2, :]
                            pe.matmul(bank, ident_b[:, :], mask_t[:, j, cut], start=True, stop=False)
                            mm = pe.matmul(bank, sel[:, 2, :], qs[:, n, cut], start=False, stop=True)
                        mm.then_inc(s_score, 1)

                    def spread_i(s):
                        n, c = s // TILES, s // BLOCKS % 2
                        pe.wait_ge(s_shift, SHIFT_CREDIT + SHIFT0[layer] + u * UNROLL + n + 1)
                        pe.wait_ge(s_si8, CREDIT + 2 * (UNIT0[layer] - UNIT0[2]) + u * (2 * UNROLL) + s // BLOCKS - 1)
                        pe.matmul(ps[:, 2 + c, :], sel[0:64, 0, :], qs[0:64, n, c * HALF:(c + 1) * HALF],
                                  start=True, stop=True).then_inc(s_si, 1)

                    def weigh(s):
                        n, tt, r = s // TILES % UNROLL, s % TILES, s % RING
                        c, j = tt // BLOCKS, tt % BLOCKS
                        H = CREDIT + 2 * UNIT0[layer] + u * (2 * UNROLL) + s // BLOCKS
                        T = tile_value(s)
                        if layer == 0:
                            if j % 2 == 0:
                                pe.wait_ge(s_chfree, CREDIT + u * (TILES // 2 * UNROLL) + s // 2 - 1)
                        elif j == 0:
                            pe.wait_ge(s_accfree, H - (0 if layer == 2 else 1) - 2 * UNITS[0])
                        pe.wait_ge(s_hi, T + 1)
                        wait_low(pe, layer, u, s)
                        for it in range(IB):
                            if layer == 0:
                                acc = ps[:, 6 + s // 2 % 2, (s % 2 * IB + it) * 33:(s % 2 * IB + it + 1) * 33]
                                opens = s % 2 == 0 and it == 0
                            elif layer == 2:
                                acc = ps[:, 6 + it // 2, it % 2 * width:(it % 2 + 1) * width]
                                opens = j == 0 and it % 2 == 0
                            else:
                                acc = ps[:, 6 + c, it * width:(it + 1) * width]
                                opens = j == 0 and it == 0
                            for h, half in enumerate((phi, plo)):
                                for v in range(3 - h):
                                    at = (j * 3 + v) * width
                                    mm = pe.matmul(acc, half[:, r, it * P:(it + 1) * P], vs[:, n, at:at + width],
                                                   start=opens and h == 0 and v == 0, stop=h == 1 and v == 1,
                                                   skip_group_check=True)
                            if layer == 3 and j == BLOCKS - 1:
                                at_i = c * HALF + it * P
                                for v in range(3):
                                    mm = pe.matmul(acc, empty[:, at_i:at_i + P], zs[:, n, v * 33:(v + 1) * 33],
                                                   start=False, stop=v == 2, skip_group_check=True)
                        mm.then_inc(s_av, 1)

                    total, lag = TILES * UNROLL, LAGS[layer]
                    for s in range(total + (lag if last else 0)):
                        n = s // TILES
                        tt = s % TILES
                        U = SHIFT0[layer] + u * UNROLL + n
                        shifts = layer and s < total
                        next_one, one_after = not (last and n == UNROLL - 1), not (last and n >= UNROLL - 2)
                        if s < total:
                            if layer > 1 and s == 0:
                                unit_ready(0, u)
                                spread_i(0)
                            scores(s)
                            if layer > 1 and s % BLOCKS == BLOCKS - 3 and s + 3 < total:
                                if s % TILES > BLOCKS:
                                    unit_ready(n + 1, u)
                                spread_i(s + 3)
                            if shifts and next_one and tt == TURN_AT[layer]:
                                turn_shift((n + 1) % UNROLL, U + 1, 2 if one_after else 0)
                        if s >= lag or not first:
                            weigh(s - lag)
                        if shifts and one_after and tt == BLOCKS - 3:
                            unit_ready((n + 2) % UNROLL, u + (n + 2) // UNROLL)
                        if layer == 1 and shifts:
                            if tt < MAX_AT and next_one:
                                top_scores((n + 1) % UNROLL, tt + TILES - MAX_AT, U + 1)
                            if tt >= MAX_AT and one_after:
                                for k in {TURN_AT[1]: (), TURN_AT[1] + 1: (3, 4)}.get(tt, (tt - MAX_AT,)):
                                    top_scores((n + 2) % UNROLL, k, U + 2)
                        if layer > 1 and shifts and one_after and tt in (BLOCKS - 3, TILES - 2):
                            spread((n + 2) % UNROLL, tt // BLOCKS, U + 2)

                if layer:
                    U = SHIFT0[layer]
                    unit_ready(0, 0)
                    if layer > 1:
                        spread(0, 0, U)
                        spread(0, 1, U)
                    else:
                        for k in range(TILES):
                            top_scores(0, k, U)
                    turn_shift(0, U)
                    unit_ready(1, 0)
                    if layer > 1:
                        spread(1, 0, U + 1)
                        spread(1, 1, U + 1)
                    else:
                        pe.wait_ge(s_shift, SHIFT_CREDIT + U + 1)
                        for k in range(TILES - MAX_AT):
                            top_scores(1, k, U + 1)
                loop(pe, layer, body)

            node(0)
            pe.wait_ge(s_mask, 2 * BLOCKS)
            heads(0)
            node(1)
            pe.wait_ge(s_krow, 1)
            heads(1)
            node(2)
            pe.wait_ge(s_mask, 4 * BLOCKS)
            pe.wait_ge(s_diag, 4 * BLOCKS)
            heads(2)
            node(3)
            pe.wait_ge(s_diag, 6 * BLOCKS)
            pe.wait_ge(s_ev["row"], ev("row", 3, GRAPHS - 1))
            for c in range(2):
                for j in range(BLOCKS):
                    mm = pe.matmul(ps[:, 4 + c, :], ones_b[:, :], mask_t[:, j, c * HALF:(c + 1) * HALF],
                                   start=j == 0, stop=j == BLOCKS - 1)
            mm.then_inc(s_cnt, 1)
            pe.wait_ge(s_empty, 1)
            heads(3)

        @block.vector
        def _(dve):
            for name in ("y", "eneg", "var", "var0", "xn", "col", "q2", "k2", "row2", "vf", "vsum", "vs"):
                dve.sem_inc(s_ev[name], 1)
            dve.sem_inc(s_shift, SHIFT_CREDIT)
            for s in (s_lo_dve, s_nmax, s_accfree, s_chfree):
                dve.sem_inc(s, CREDIT)
            dve.memset(ones_b[:, :], 1.0).then_inc(s_fill, 1)
            dve.memset(ln2[:, :], LN2).then_inc(s_fill, 1)
            dve.memset(vbuf[:, :, :, :, :], 0.0).then_inc(s_fill, 1)
            dve.memset(v2buf[:, :, :, :], 0.0).then_inc(s_fill, 1)
            dve.memset(vsumb[:, :, :, :], 0.0).then_inc(s_fill, 1)
            dve.wait_ge(s_fill, 5)
            dve.memset(vbuf[:, :, :, 0, 32], 1.0).then_inc(s_fill, 1)
            dve.memset(v2buf[:, :, 0, 128], 1.0).then_inc(s_fill, 1)
            dve.memset(vsumb[:, :, 0, 32], float(BLOCKS)).then_inc(s_fill, 1)
            dve.wait_ge(s_fill, 8)
            dve.wait_ge(s_ident, 5)
            dve.memset(sel[:, :, :].bitcast(F32), 0.0).then_inc(s_sel, 1)
            dve.wait_ge(s_sel, 1)
            dve.memset(sel[0:2, 0, :].bitcast(F32), 1.0).then_inc(s_sel, 1)
            dve.memset(sel[32:34, 1, :].bitcast(F32), 1.0).then_inc(s_sel, 1)
            dve.memset(sel[96:97, 2, :].bitcast(F32), 1.0).then_inc(s_sel, 1)
            dve.memset(sel[64:66, 2, :].bitcast(F32), 1.0).then_inc(s_sel, 1)
            dve.wait_ge(s_const, 16 * 22)

            def node(stage):
                state = {}

                def link(ins):
                    state["n"] += 1
                    ins.then_inc(state["signal"], 1)
                    dve.wait_ge(state["signal"], state["base"] + state["n"])

                def begin(signal, counts, b):
                    state.update(n=0, signal=signal, base=GRAPHS * sum(counts[:stage]) + b * counts[stage])

                def end(counts):
                    assert state["n"] == counts[stage], (stage, counts, state["n"])

                def row(k):
                    return rows[:, k, :].unsqueeze(1).to_broadcast([P, BLOCKS, F])

                def done(name, b, ins):
                    ins.then_inc(s_ev[name], 1)
                    dve.wait_ge(s_ev[name], ev(name, stage, b))

                def layer_norm(dst, name, b):
                    for it in range(BLOCKS):
                        ins = dve.bn_stats(bns[:, it, :], work[:, it, :])
                    link(ins)
                    dve.sem_inc(s_carry, 1)
                    for it in range(BLOCKS):
                        ins = dve.bn_aggr(mv[:, it, :], bns[:, it, :])
                    link(ins)
                    dve.tensor_scalar(var[:, :], mv[:, :, 1], EPS, None, ALU.add).then_inc(s_ev["var" + name], 1)
                    dve.wait_ge(s_ev["rstd" + name], ev("rstd" + name, stage, b))
                    for it in range(BLOCKS):
                        ins = dve.tensor_scalar(dst[:, it, :], work[:, it, :], mv[:, it, 0:1], rstd[:, it:it + 1],
                                                ALU.subtract, ALU.mult)
                    return ins

                def finish(b, q, h):
                    if stage == 0:
                        return
                    begin(s_chain_a, CHAIN_A, b)
                    w, x = work[:, :, :], xr[:, q, :, :]
                    if stage in (1, 2):
                        dve.wait_ge(s_load[q], load_at(stage, h))
                        dve.wait_ge(s_ev["y_ps"], ev("y_ps", stage, b))
                        y = pf[:, 2 * HALF:4 * HALF].rearrange("p (t f) -> p t f", f=F)
                        done("y", b, dve.tensor_tensor(w, y, row(2 * stage - 1), ALU.add))
                        link(dve.tensor_tensor(w, w, x, ALU.add))
                    if stage == 1:
                        link(layer_norm(work, "0", b))
                        link(dve.tensor_tensor(w, w, row(4), ALU.mult))
                        link(dve.tensor_tensor(w, w, row(5), ALU.add))
                        link(dve.tensor_tensor(w, w, x, ALU.add))
                    if stage in (3, 4):
                        dve.wait_ge(s_load[q], load_at(stage, h))
                        c = cs[:, q, :, :]
                        dve.tensor_scalar(neg[:, :, :], c, 0.0, None, ALU.min).then_inc(s_ev["eneg"], 1)
                        dve.wait_ge(s_ev["eexp"], ev("eexp", stage, b))
                        link(dve.scalar_tensor_tensor(w, c, 0.0, neg[:, :, :], ALU.max, ALU.add))
                        link(dve.scalar_tensor_tensor(w, w, -1.0, x, ALU.add, ALU.add))
                    dve.wait_ge(s_xst[q], xst_before(stage, h))
                    if stage < 4:
                        dve.wait_ge(s_ev["xT_ps"], before("xT_ps", stage, b) - 1)
                    done("xn", b, layer_norm(xn[:, q, :, :], "", b))
                    end(CHAIN_A)

                def make_masks(b, q, h):
                    for k, mask in enumerate((mask_t, mask_n)):
                        dve.wait_ge(s_adj[2 * q + k], 16 * (GRAPHS // 4 * stage + 1) + h * 16)
                        dve.tensor_scalar(mask[:, bass.ds(b, 1), :].rearrange("p a n -> p (a n)"),
                                          adj_i[:, 2 * q + k, :], 0.0, -BIG,
                                          ALU.is_le if stage else ALU.is_equal, ALU.mult).then_inc(s_mask, 1)

                def project(b, q, h):
                    if stage == 4:
                        return
                    begin(s_chain_b, CHAIN_B, b)
                    dve.wait_ge(s_ev["v_ps"], ev("v_ps", stage, b))
                    dve.wait_ge(s_ev["v"], before("v", stage, b))
                    v = pf[:, 2 * HALF:4 * HALF].rearrange("p (t f) -> p t f", f=F)
                    if stage < 2:
                        dve.tensor_tensor(vf[:, :, :], v, row(2 * stage), ALU.add).then_inc(s_ev["vf"], 1)
                    else:
                        done("vf", b, dve.tensor_copy(vf[:, :, :], v))
                    if stage == 3:
                        done("vsum", b, dve.tensor_reduce(vsum[:, :], vf[:, :, :].rearrange("p t f -> p f t"),
                                                          AX.X, ALU.add))
                    dve.wait_ge(s_rst[q], rst_before(stage, h))
                    if stage < 2:
                        for w, name in enumerate("qk"):
                            dve.wait_ge(s_ev[name], ev(name, stage, b))
                            dve.scalar_tensor_tensor(
                                part[:, q, w, 1, :], pf[:, (6 - 2 * w) * HALF:(8 - 2 * w) * HALF],
                                bcol[:, 2 * stage + w:2 * stage + w + 1], part[:, q, w, 0, :].bitcast(F32),
                                ALU.add, ALU.subtract).then_inc(s_ev[name + "2"], 1)
                        if stage == 0:
                            make_masks(b, q, h)
                        return
                    if stage == 2:
                        make_masks(b, q, h)
                    n = 2 * HEADS[stage]
                    dve.wait_ge(s_pst, pst_before(stage, b))
                    dve.wait_ge(s_ev["row"], ev("row", stage, b))
                    done("col", b, dve.tensor_copy(
                        colp[:, 0:n, :], ps[:, 0, 0:BLOCKS * n].rearrange("p (t r) -> p r t", r=n)))
                    r = full[0:n, 1, :]
                    link(dve.tensor_copy(rowp[0:n, q, 0, :], r))
                    link(dve.tensor_tensor(rowp[0:n, q, 1, :], r, rowp[0:n, q, 0, :].bitcast(F32), ALU.subtract))
                    link(dve.tensor_scalar(r, r, SLOPE, None, ALU.mult))
                    link(dve.tensor_copy(rowp[0:n, q, 2, :], r))
                    dve.tensor_tensor(rowp[0:n, q, 3, :], r, rowp[0:n, q, 2, :].bitcast(F32), ALU.subtract
                                      ).then_inc(s_ev["row2"], 1)
                    if stage == 3:
                        z, zf = (lambda s: vsumb[:, :, s, 0:32]), vsum[:, :].rearrange("p (h d) -> p h d", h=4)
                        link(dve.tensor_copy(z(0), zf))
                        link(dve.tensor_tensor(zf, zf, z(0), ALU.subtract))
                        link(dve.tensor_copy(z(1), zf))
                        dve.tensor_tensor(z(2), zf, z(1), ALU.subtract).then_inc(s_ev["vs"], 1)
                    end(CHAIN_B)

                graphs(dve, finish, project)

            def heads(layer):
                width = WIDTH[layer]
                per = HCHAIN[layer]
                chain0 = sum(HCHAIN[m] * UNITS[m] // UNROLL for m in range(layer))
                state = {}

                def link(ins):
                    state["n"] += 1
                    ins.then_inc(s_hchain, 1)
                    dve.wait_ge(s_hchain, state["base"] + state["n"])

                def find_shift(n, U):
                    M, z, l = shift[:, 0, :], shift[:, 1, :], shift[:, 2, :]
                    link(dve.tensor_reduce(M, top[:, :, :], AX.X, ALU.max))
                    if layer == 1:
                        dve.tensor_scalar(nshift[:, n % 2, :], M, LEAST, -1.0, ALU.max, ALU.mult
                                          ).then_inc(s_shcol, 1)
                    else:
                        link(dve.tensor_tensor(z, M, cols[:, n, 0, :], ALU.add))
                        link(dve.tensor_scalar(z, z, LEAST, None, ALU.max))
                        link(dve.tensor_scalar(l, z, SLOPE, None, ALU.mult))
                        link(dve.tensor_tensor(l, z, l, ALU.max))
                        dve.tensor_scalar(nshift[:, n % 2, :], l, -1.0, None, ALU.mult).then_inc(s_shcol, 1)
                        dve.tensor_scalar(colx[:, n, :], cols[:, n, 1, :], SLOPE - 1.0, None, ALU.mult
                                          ).then_inc(s_colx, 1)
                        dve.wait_ge(s_colx, U - SHIFT0[2] + 1)

                def shift_rows(n, U):
                    dve.wait_ge(s_shT, U + 1)
                    dve.tensor_copy(shrow[:, n % 2, :], ps[0:BLOCKS, TURN_BANK[layer], 0:P]).then_inc(s_shift, 1)

                def take_max(k, U):
                    dve.wait_ge(s_nmax, CREDIT + TILES * U + k)
                    if layer == 1:
                        it, c = k // 2, k % 2
                        dve.wait_ge(s_nsc, TILES * U + k + 1)
                    else:
                        it, c = k % BLOCKS, k // BLOCKS
                        dve.wait_ge(s_nsc, (TILES - 2) * SHIFT0[2] + 2 * U + c + 1)
                    dve.sem_inc(s_carry, 1)
                    dve.tensor_tensor_reduce(junk[:, :], ps[:, 4 + c, :], mask_n[:, it, c * HALF:(c + 1) * HALF],
                                             1.0, LOWEST, ALU.add, ALU.max,
                                             accum_out=top[:, it, c:c + 1]).then_inc(s_nmax, 1)
                    if k == TILES - 1:
                        dve.wait_ge(s_nmax, CREDIT + TILES * U + TILES)

                def body(u, first, last):
                    state["n"] = 0
                    state["base"] = chain0 + HPRE[layer] + (0 if first else u * per - HLEFT[layer])

                    def tile_value(s):
                        return CREDIT + TILES * UNIT0[layer] + u * (TILES * UNROLL) + s

                    def settle(s):
                        T, r = tile_value(s), s % RING
                        if layer == 0:
                            dve.wait_ge(s_exp, T + 1)
                            p = prob[:, r, :]
                            dve.tensor_scalar(p, p, CLIP_LO, CLIP_HI, ALU.max, ALU.min).then_inc(s_p, 1)
                        else:
                            n, c, j = s // TILES, s // BLOCKS % 2, s % BLOCKS
                            if j == 0:
                                dve.wait_ge(s_si8, CREDIT + 2 * (UNIT0[layer] - UNIT0[2]) + u * (2 * UNROLL)
                                            + s // BLOCKS + 1)
                            dve.wait_ge(s_score, T - CREDIT + 1)
                            dve.wait_ge(s_hi, T - RING + 1)
                            dve.scalar_tensor_tensor(arg[:, r, :], si8[:, c * HALF:(c + 1) * HALF],
                                                     colx[:, n, j:j + 1], ps[:, s % 2, :], ALU.max, ALU.add
                                                     ).then_inc(s_p, 1)

                    def out_free(n):
                        dve.wait_ge(s_ctx[n % 2], stored_before(layer, u, n))

                    def blocks_done(s):
                        n, tt = s // TILES, s % TILES
                        c, j = tt // BLOCKS, tt % BLOCKS
                        acc = ps[:, 6 + s // 2 % 2, 0:2 * IB * 33].rearrange("p (a d) -> p a d", d=33)
                        dve.wait_ge(s_av, tile_value(s) + 1)
                        dve.wait_ge(s_chfree, CREDIT + u * (TILES // 2 * UNROLL) + s // 2)
                        link(dve.reciprocal(rden[:, 0:2 * IB], acc[:, :, 32]))
                        dve.tensor_tensor(blk[:, j - 1:j + 1, :, :].rearrange("p j t d -> p (j t) d"), acc[:, :, 0:32],
                                          rden[:, 0:2 * IB].unsqueeze(2).to_broadcast([P, 2 * IB, 32]),
                                          ALU.mult).then_inc(s_chfree, 1)
                        if j == BLOCKS - 1:
                            dve.wait_ge(s_chfree, CREDIT + u * (TILES // 2 * UNROLL) + s // 2 + 1)
                            U = UNIT0[layer] + u * UNROLL + n
                            if c == 0:
                                out_free(n)
                            ins = dve.tensor_reduce(
                                outp[:, n % 2, c * IB * 32:(c + 1) * IB * 32].rearrange("p (t d) -> p t d", d=32),
                                blk[:, :, :, :].rearrange("p j t d -> p t d j"), AX.X, ALU.add)
                            if c == 1:
                                ins.then_inc(s_out, 1)
                                dve.wait_ge(s_out, U + 1)
                            else:
                                link(ins)

                    def half_done(s):
                        n, tt = s // TILES, s % TILES
                        c = tt // BLOCKS
                        U = UNIT0[layer] + u * UNROLL + n
                        dve.wait_ge(s_av, tile_value(s) + 1)
                        if c == 0:
                            out_free(n)
                        banks = ((6, 2), (7, 2)) if layer == 2 else ((6 + c, IB),)
                        for m, (bank, blocks) in enumerate(banks):
                            acc = ps[:, bank, 0:blocks * (width + 1)].rearrange("p (t d) -> p t d", d=width + 1)
                            link(dve.tensor_scalar(rden[:, 0:blocks], acc[:, :, width], TINY, None, ALU.max))
                            link(dve.reciprocal(rden[:, 0:blocks], rden[:, 0:blocks]))
                            at = (c * IB + m * 2) * width
                            link(dve.tensor_tensor(
                                outp[:, n % 2, at:at + blocks * width].rearrange("p (t d) -> p t d", d=width),
                                acc[:, :, 0:width],
                                rden[:, 0:blocks].unsqueeze(2).to_broadcast([P, blocks, width]), ALU.mult))
                        dve.sem_inc(s_accfree, 1)
                        if c == 1:
                            dve.sem_inc(s_out, 1)

                    total, lag = TILES * UNROLL, LAGS[layer]
                    for s in range(total + (lag + 1 if last else 0)):
                        if s < total and layer != 1:
                            settle(s)
                        if s <= total and (s or not first) and (s - 1) % RING in DVE_LOW[layer]:
                            take_low(dve, layer, u, s - 1)
                        n = s // TILES
                        if layer and s < total:
                            tt, U = s % TILES, SHIFT0[layer] + u * UNROLL + n
                            next_one, one_after = not (last and n == UNROLL - 1), not (last and n >= UNROLL - 2)
                            if tt == TURN_AT[layer] and next_one:
                                shift_rows((n + 1) % UNROLL, U + 1)
                            if tt <= MAX_AT and next_one:
                                take_max(tt + TILES - MAX_AT - 1, U + 1)
                                if tt == MAX_AT:
                                    find_shift((n + 1) % UNROLL, U + 1)
                            if tt > MAX_AT and one_after:
                                take_max(tt - MAX_AT - 1, U + 2)
                        e = s - lag - 1
                        if e >= 0 or not first:
                            if layer == 0 and e % 2:
                                blocks_done(e)
                            if layer and e % BLOCKS == BLOCKS - 1:
                                half_done(e)
                    want = per - (HPRE[layer] if last else 0) + HLEFT[layer] * (last - first)
                    assert state["n"] == want, (layer, first, last, state["n"], want)

                if layer:
                    state["n"], state["base"] = 0, chain0
                    dve.wait_ge(s_stk[0], stk_at(layer, 0, 0))
                    for k in range(TILES):
                        take_max(k, SHIFT0[layer])
                    find_shift(0, SHIFT0[layer])
                    shift_rows(0, SHIFT0[layer])
                    for k in range(TILES - MAX_AT - 1):
                        take_max(k, SHIFT0[layer] + 1)
                    assert state["n"] == HPRE[layer]
                loop(dve, layer, body)

            node(0)
            heads(0)
            node(1)
            heads(1)
            node(2)
            heads(2)
            node(3)
            dve.wait_ge(s_cnt, 1)
            dve.tensor_scalar(empty[:, :], pf[:, 4 * HALF:6 * HALF], -BIG * NODES, None, ALU.is_equal
                              ).then_inc(s_empty, 1)
            heads(3)
            node(4)


_WEIGHTS = ("L0_gnn_Wq", "L0_gnn_Wk", "L0_gnn_Wv", "L0_gnn_Wo", "L1_gnn_wq", "L1_gnn_wk", "L1_gnn_wv", "L1_gnn_wo")
_ROWS = ("L0_gnn_bv", "L0_gnn_bo", "L1_gnn_bv", "L1_gnn_bo", "L0_gnn_gamma", "L0_gnn_beta")
_COLS = ("L0_gnn_bq", "L0_gnn_bk", "L1_gnn_bq", "L1_gnn_bk")


def kernel(**inputs):
    import numpy as np
    import concourse.bacc as bacc
    from concourse import mybir as _mybir
    from concourse.bass_utils import run_bass_kernel_spmd

    a = {n: np.asarray(v) for n, v in inputs.items()}
    arrays = {"x": a["x"], "adj_n": a["adj"], "adj_t": a["adj"].T}
    for n in _WEIGHTS:
        arrays[n] = a[n].T
    for n in _ROWS:
        arrays[n] = np.broadcast_to(a[n], (P, F))
    for n in _COLS:
        arrays[n] = a[n].reshape(F, 1)
    arrays["L2_gnn_W"] = a["L2_gnn_W"]
    arrays["L2_gnn_a"] = a["L2_gnn_a"].reshape(2, F).T
    arrays["L3_gnn_W"] = a["L3_gnn_W"].transpose(1, 0, 2).reshape(F, F)
    side = np.zeros((4, 32, 2, 4), a["L3_gnn_a"].dtype)
    for h in range(4):
        side[h, :, 0, h] = a["L3_gnn_a"][h, :32]
        side[h, :, 1, h] = a["L3_gnn_a"][h, 32:]
    arrays["L3_gnn_a"] = side.reshape(F, 8)
    arrays = {n: np.ascontiguousarray(v) for n, v in arrays.items()}

    nc = bacc.Bacc("TRN2", target_bir_lowering=False, num_devices=1)
    t = {n: nc.dram_tensor("in_" + n, v.shape, _mybir.dt.from_np(v.dtype), kind="ExternalInput").ap()
         for n, v in arrays.items()}
    t["out"] = nc.dram_tensor("out_0", (GRAPHS, NODES, F), F32, kind="ExternalOutput").ap()
    build(nc, t)
    r = run_bass_kernel_spmd(nc, [{"in_" + n: v for n, v in arrays.items()}], core_ids=[0])
    return r.results[0]["out_0"]
```
